# Optimizing a Trainium2 kernel written in Bass

```python
import numpy as np
import jax
import jax.numpy as jnp

def _softmax(x, axis=-1):
    return jax.nn.softmax(x, axis=axis)

def _gelu(x):
    return jax.nn.gelu(x, approximate=True)

def _silu(x):
    return jax.nn.silu(x)

def _sigmoid(x):
    return jax.nn.sigmoid(x)

def _layernorm(x, axis=-1, eps=1e-05):
    m = jnp.mean(x, axis=axis, keepdims=True)
    v = jnp.var(x, axis=axis, keepdims=True)
    return (x - m) / jnp.sqrt(v + eps)

def _scatter_add(tgt, idx, src, axis=0):
    return tgt.at[idx].add(src)

def _segment_sum(src, seg, n):
    return jax.ops.segment_sum(src, seg, n)
kernel_name = 'mk_gnn_preln_d1_gnn_r16_14283c'

def setup_inputs(seed: int=0):
    np.random.seed(seed)
    _w = jnp.asarray

    def _rec_inputs():
        import jax
        import jax.numpy as jnp
        _gk = jax.random.key(seed)
        x = -0.000202 + 1 * jax.random.normal(jax.random.fold_in(_gk, 1), (6250, 128), jnp.float32)
        src = jax.random.randint(jax.random.fold_in(_gk, 2), (200000,), 0, 6250, jnp.int32)
        dst = jnp.minimum((6250 * jax.random.uniform(jax.random.fold_in(_gk, 3), (200000,)) ** 2.0).astype(jnp.int32), 99999)
        _o = jnp.argsort(dst, stable=True)
        src = src[_o]
        dst = dst[_o]
        return (x, src, dst)
    x, src, dst = _rec_inputs()

    def _L0_gnn_setup():
        import jax, jax.numpy as jnp
        import numpy as np
        N = 3125
        E = 50000
        DIN = 128
        H = 256
        DOUT = 128
        NEG_SLOPE = 0.01

        def _lin(key, din, dout):
            return jax.random.normal(key, (din, dout), jnp.float32) * (1.0 / np.sqrt(din))

        def _sage_conv(x, src, dst, Wl, bl, Wr):
            agg = jax.ops.segment_max(x[src], dst, num_segments=x.shape[0])
            agg = jnp.where(jnp.isfinite(agg), agg, 0.0)
            return agg @ Wl + bl + x @ Wr
        key = jax.random.key(seed)
        ks = jax.random.split(key, 10)
        return {'x': jax.random.normal(ks[0], (N, DIN), jnp.float32), 'edge_index': jax.random.randint(ks[1], (2, E), 0, N, dtype=jnp.int64), 'Wl1': _lin(ks[2], DIN, H), 'bl1': jnp.zeros((H,), jnp.float32), 'Wr1': _lin(ks[3], DIN, H), 'Wl2': _lin(ks[4], H, H), 'bl2': jnp.zeros((H,), jnp.float32), 'Wr2': _lin(ks[5], H, H), 'Wl3': _lin(ks[6], H, DOUT), 'bl3': jnp.zeros((DOUT,), jnp.float32), 'Wr3': _lin(ks[7], H, DOUT)}
    _L0_gnn_all = _L0_gnn_setup()
    _L0_gnn_in = {k: v for k, v in _L0_gnn_all.items() if k in ('Wl1', 'bl1', 'Wr1', 'Wl2', 'bl2', 'Wr2', 'Wl3', 'bl3', 'Wr3')}
    del _L0_gnn_all
    return {'x': x, 'src': src, 'dst': dst, 'L0_gnn_Wl1': _L0_gnn_in['Wl1'], 'L0_gnn_bl1': _L0_gnn_in['bl1'], 'L0_gnn_Wr1': _L0_gnn_in['Wr1'], 'L0_gnn_Wl2': _L0_gnn_in['Wl2'], 'L0_gnn_bl2': _L0_gnn_in['bl2'], 'L0_gnn_Wr2': _L0_gnn_in['Wr2'], 'L0_gnn_Wl3': _L0_gnn_in['Wl3'], 'L0_gnn_bl3': _L0_gnn_in['bl3'], 'L0_gnn_Wr3': _L0_gnn_in['Wr3']}

def reference(x, src, dst, L0_gnn_Wl1, L0_gnn_bl1, L0_gnn_Wr1, L0_gnn_Wl2, L0_gnn_bl2, L0_gnn_Wr2, L0_gnn_Wl3, L0_gnn_bl3, L0_gnn_Wr3):
    import jax
    import jax.numpy as jnp

    def _L0_gnn_ref(x, edge_index, Wl1, bl1, Wr1, Wl2, bl2, Wr2, Wl3, bl3, Wr3):
        import jax, jax.numpy as jnp
        import numpy as np
        N = 3125
        E = 50000
        DIN = 128
        H = 256
        DOUT = 128
        NEG_SLOPE = 0.01

        def _lin(key, din, dout):
            return jax.random.normal(key, (din, dout), jnp.float32) * (1.0 / np.sqrt(din))

        def _sage_conv(x, src, dst, Wl, bl, Wr):
            agg = jax.ops.segment_max(x[src], dst, num_segments=x.shape[0])
            agg = jnp.where(jnp.isfinite(agg), agg, 0.0)
            return agg @ Wl + bl + x @ Wr
        src, dst = (edge_index[0], edge_index[1])
        h = jax.nn.leaky_relu(_sage_conv(x, src, dst, Wl1, bl1, Wr1), NEG_SLOPE)
        h = jax.nn.leaky_relu(_sage_conv(h, src, dst, Wl2, bl2, Wr2), NEG_SLOPE)
        h = jax.nn.leaky_relu(_sage_conv(h, src, dst, Wl3, bl3, Wr3), NEG_SLOPE)
        return h
    edge_index = jnp.stack([src, dst])
    h = jnp.maximum(_layernorm(x, axis=-1), 0.0)
    x = x + _L0_gnn_ref(h, edge_index, L0_gnn_Wl1, L0_gnn_bl1, L0_gnn_Wr1, L0_gnn_Wl2, L0_gnn_bl2, L0_gnn_Wr2, L0_gnn_Wl3, L0_gnn_bl3, L0_gnn_Wr3)
    return x

_drawn_inputs = setup_inputs


def setup_inputs(seed=0):
    import zlib

    import numpy as np

    out = dict(_drawn_inputs(seed))
    spreads = {'L0_gnn_bl1': (0.0, 0.27), 'L0_gnn_bl2': (0.0, 0.1), 'L0_gnn_bl3': (0.0, 0.285)}
    factors = {}
    for name, (base, spread) in spreads.items():
        noise = np.random.default_rng([zlib.crc32(name.encode()), seed]).standard_normal(out[name].shape)
        drawn = base * np.exp(spread * noise) if base else spread * noise
        out[name] = jnp.asarray(drawn.astype(out[name].dtype))
    for name, factor in factors.items():
        out[name] = (out[name] * factor).astype(out[name].dtype)
    return out
```

```python
from contextlib import ExitStack

import concourse.bass as bass
from concourse import mybir

ALU = mybir.AluOpType
ACT = mybir.ActivationFunctionType
AXIS = mybir.AxisListType
F32 = mybir.dt.float32
BF16 = mybir.dt.bfloat16
I32 = mybir.dt.int32
U32 = mybir.dt.uint32

P = 128
LANE_BITS = 7
BLOCKS = 3
BLOCK_COLS = 18
RING_COLS = BLOCKS * BLOCK_COLS
HALF = 5
TAIL_TILES = 2 * HALF
OUT_RING = 5
DMA = 16
LOWEST = -3.4028234663852886e38
TOP_EXPONENT = 0x7F000000
SLOPE = 0.01
EPS = 1e-5
NO_NODE = 1 << 20


def gnn_program(nc, x, src, dst, weights, out):
    NODES, F_IN = x.shape
    COLS = src.shape[1]
    TILES = NODES // P
    STEPS = COLS // RING_COLS
    TAIL_STEPS = TILES // TAIL_TILES
    PAIRS = TILES // 2
    assert COLS % RING_COLS == 0 and TILES % TAIL_TILES == 0 and TAIL_TILES % OUT_RING == 0
    assert PAIRS <= STEPS
    shapes = [wl.shape for wl, _, _ in weights]
    F_MAX = max(max(s) for s in shapes)
    KC_MAX = F_MAX // P
    LOG_ROWS = P * COLS + 1
    SCANS_STEP = RING_COLS + 1
    SCANS = STEPS * SCANS_STEP
    STAGED = STEPS * BLOCKS + BLOCKS

    tables = [nc.dram_tensor(f"features_{l}", (NODES, s[0]), F32).ap() for l, s in enumerate(shapes)]
    widths = sorted({s[0] for s in shapes})
    logs = {w: nc.dram_tensor(f"running_max_log_{w}", (LOG_ROWS, w), F32).ap() for w in widths}

    with ExitStack() as ctx:
        def sb(name, shape, dt=F32):
            return ctx.enter_context(nc.sbuf_tensor(name, shape, dt))

        def ps(name, shape, dt=F32):
            return ctx.enter_context(nc.psum_tensor(name, shape, dt))

        def sem(name):
            return ctx.enter_context(nc.semaphore(name))

        ring = sb("ring", [P, RING_COLS * F_MAX])
        second = RING_COLS * F_IN
        x_all = ring[:, 0:TILES * F_IN].rearrange("p (t f) -> p t f", f=F_IN)
        h0_all = ring[:, second:second + TILES * F_IN].rearrange("p (t f) -> p t f", f=F_IN)
        HOT = P + TILES
        HOT_WORDS = RING_COLS * HOT // 2
        assert second >= TILES * F_IN and second + max(TILES * F_IN, HOT_WORDS) <= RING_COLS * F_MAX
        hot = ring[:, second:second + HOT_WORDS].bitcast(BF16).rearrange("p (c h) -> p c h", h=HOT)

        own = sb("own", [P, TILES * F_MAX])
        src_t = sb("src_t", [P, COLS + RING_COLS], I32)
        dst_t = sb("dst_t", [P, COLS], I32)
        restart = sb("restart", [P, COLS])
        dst_lane = sb("dst_lane", [P, COLS], BF16)
        dst_tile = sb("dst_tile", [P, COLS], BF16)
        index_stage = sb("index_stage", [P, BLOCKS, BLOCK_COLS], I32)
        end_row = sb("end_row", [P, TILES + TAIL_TILES], I32)
        end_stage = sb("end_stage", [P, 2, HALF], I32)
        wl_sb, wr_sb, b_sb = [], [], []
        for l, (k, n) in enumerate(shapes):
            wl_sb.append(sb(f"wl{l}", [P, k // P, n]))
            wr_sb.append(sb(f"wr{l}", [P, k // P, n]))
            b_sb.append(sb(f"b{l}", [1, n]))
        lane_i = sb("lane_i", [P, P], I32)
        lane = sb("lane", [P, P])
        lane_bf = sb("lane_bf", [P, P], BF16)
        part_i = sb("part_i", [P, 2], I32)
        part = sb("part", [P, 2])
        ident = sb("ident", [P, P])
        upper = sb("upper", [P, P])
        ones = sb("ones", [P, P])
        prev_last = sb("prev_last", [P, 1], I32)
        cols = sb("cols", [P, 8])
        patch_row = sb("patch_row", [P, 1], I32)
        diag = sb("diag", [P, 2, P])
        join_row = sb("join_row", [P, 2, P])
        stats = sb("stats", [P, TAIL_TILES, 6])
        mean_var = sb("mean_var", [P, TILES, 2])
        std = sb("std", [P, TILES])
        rstd = sb("rstd", [P, TILES])
        shift = sb("shift", [P, TILES])
        eps = sb("eps", [P, 1])
        count = sb("count", [P, TILES])
        total = sb("total", [P, TILES])
        empty_row = sb("empty_row", [1, F_MAX])
        no_hot = sb("no_hot", [P, HOT], BF16)
        upto = sb("upto", [P, TILES])
        ends = sb("ends", [P, TILES])
        zero_tiles = sb("zero_tiles", [P, TILES])
        h_in = [sb(f"h_in{b}", [P, F_MAX]) for b in range(2)]
        h_turned = [sb(f"h_turned{b}", [P, KC_MAX, P]) for b in range(2)]
        agg = [sb(f"agg{b}", [P, KC_MAX * P]) for b in range(2)]
        finite = [sb(f"finite{b}", [P, KC_MAX * P], I32) for b in range(2)]
        z_sum = [sb(f"z_sum{b}", [P, F_MAX]) for b in range(2)]
        h_out = [sb(f"h_out{b}", [P, F_MAX]) for b in range(OUT_RING)]
        carry = sb("carry", [P, F_MAX])
        carry_scan = sb("carry_scan", [P, KC_MAX, P])
        incoming = sb("incoming", [P, KC_MAX, P])
        patch = sb("patch", [P, F_MAX])

        hist_ps = ps("hist_ps", [P, 512])
        turn_ps = [ps(f"turn_ps{b}", [P, 512]) for b in range(2)]
        mm_ps = [ps(f"mm_ps{b}", [P, 512]) for b in range(2)]
        carry_ps = ps("carry_ps", [P, 512])
        back_ps = ps("back_ps", [P, 512])

        x_loaded = [sem(f"x_loaded{s}") for s in range(TAIL_STEPS)]
        edges_loaded, weights_loaded = sem("edges_loaded"), sem("weights_loaded")
        iota_done, const_done, prep_done = sem("iota_done"), sem("const_done"), sem("prep_done")
        stats_done, var_done, std_done, norm_ready = (
            sem("stats_done"), sem("var_done"), sem("std_done"), sem("norm_ready"))
        h0_done, h0_stored, empty_stored = sem("h0_done"), sem("h0_stored"), sem("empty_stored")
        join_diag, join_spread = sem("join_diag"), sem("join_spread")
        index_staged, gathers_open = sem("index_staged"), sem("gathers_open")
        landed = [sem(f"landed{b}") for b in range(BLOCKS)]
        scan_done = sem("scan_done")
        logged = [sem(f"logged{b}") for b in range(BLOCKS)]
        hot_ready, hot_used = sem("hot_ready"), [sem(f"hot_used{b}") for b in range(BLOCKS)]
        count_ready, count_spread, ends_step = sem("count_ready"), sem("count_spread"), sem("ends_step")
        in_loaded = [sem(f"in_loaded{b}") for b in range(2)]
        in_turned, in_copied, own_mm, own_done = (
            sem("in_turned"), sem("in_copied"), sem("own_mm"), sem("own_done"))
        carry_turned, join_step, incoming_ready, incoming_turned = (
            sem("carry_turned"), sem("join_step"), sem("incoming_ready"), sem("incoming_turned"))
        patch_landed, patched, patch_stored = sem("patch_landed"), sem("patched"), sem("patch_stored")
        end_staged = sem("end_staged")
        end_landed = [sem(f"end_landed{k}") for k in range(TAIL_TILES)]
        agg_turned, mask_done, guard_open, agg_done = (
            sem("agg_turned"), sem("mask_done"), sem("guard_open"), sem("agg_done"))
        z_ready, sum_done, act_done, h_done = (
            sem("z_ready"), sem("sum_done"), sem("act_done"), sem("h_done"))
        h_stored = [sem(f"h_stored{b}") for b in range(OUT_RING)]
        residual_loaded = sem("residual_loaded")

        LAYERS = len(shapes)
        CONSTS = 14
        PREP = 14
        ENDS = 6
        N_WEIGHTS = 3 * LAYERS * DMA
        PER_OUT = TILES // OUT_RING * DMA

        def log_block(l, step, b):
            w = shapes[l][0]
            body = logs[w][0:P * COLS, :].rearrange("(p c) f -> p (c f)", p=P)
            return body[:, bass.ds((step * BLOCKS + b) * (BLOCK_COLS * w), BLOCK_COLS * w)]

        block = ctx.enter_context(nc.Block())

        @block.gpsimd
        def _(pool):
            pool.iota(lane_i[:, :], [[1, P]], base=0, channel_multiplier=0).then_inc(iota_done, 1)
            pool.iota(part_i[:, 0:1], [[0, 1]], base=0, channel_multiplier=1).then_inc(iota_done, 1)
            pool.iota(part_i[:, 1:2], [[0, 1]], base=0, channel_multiplier=COLS).then_inc(iota_done, 1)

            for l, (w, _n) in enumerate(shapes):
                if l == 0:
                    pool.wait_ge(h0_stored, DMA * TAIL_STEPS)
                else:
                    for b in range(OUT_RING):
                        pool.wait_ge(h_stored[b], PER_OUT * l)
                def gather(i, first):
                    for b in range(BLOCKS):
                        pool.wait_ge(index_staged, i * BLOCKS + (STAGED * l + b + 1))
                        if not first:
                            pool.wait_ge(logged[b], i * DMA + DMA * STEPS * l)
                        pool.sem_inc(gathers_open, 1)
                        for u in range(BLOCK_COLS):
                            c = b * BLOCK_COLS + u
                            pool.indirect_dma_start(
                                ring[:, c * w:(c + 1) * w], None, tables[l],
                                bass.IndirectOffsetOnAxis(
                                    ap=index_stage[:, b, u:u + 1].bitcast(U32), axis=0),
                            ).then_inc(landed[b], DMA)

                if l == 0:
                    gather(0, True)
                with pool.Fori(1 if l == 0 else 0, STEPS) as i:
                    gather(i, False)
                for b in range(BLOCKS):
                    pool.wait_ge(logged[b], DMA * STEPS * (l + 1))
                pool.wait_ge(prep_done, PREP)
                pool.indirect_dma_start(
                    patch[:, 0:w], None, logs[w],
                    bass.IndirectOffsetOnAxis(ap=patch_row[:, 0:1].bitcast(U32), axis=0),
                ).then_inc(patch_landed, DMA)
                pool.wait_ge(patched, l + 1)
                pool.indirect_dma_start(
                    logs[w], bass.IndirectOffsetOnAxis(ap=patch_row[:, 0:1].bitcast(U32), axis=0),
                    patch[:, 0:w], None,
                ).then_inc(patch_stored, DMA)
                pool.wait_ge(patch_stored, DMA * (l + 1))
                pool.wait_ge(empty_stored, DMA * len(widths))
                with pool.Fori(0, TAIL_STEPS) as i:
                    for k in range(TAIL_TILES):
                        if k % HALF == 0:
                            pool.wait_ge(end_staged, i * 2 + (2 * (TAIL_STEPS + 1) * l + k // HALF + 1))
                            pool.sem_inc(gathers_open, 1)
                        pool.indirect_dma_start(
                            ring[:, k * w:(k + 1) * w], None, logs[w],
                            bass.IndirectOffsetOnAxis(
                                ap=end_stage[:, k // HALF, k % HALF:k % HALF + 1].bitcast(U32), axis=0),
                        ).then_inc(end_landed[k], DMA)

        @block.vector
        def _(dve):
            dve.memset(ones[:, :], 1.0).then_inc(const_done, 1)
            dve.memset(eps[:, :], EPS).then_inc(const_done, 1)
            dve.memset(zero_tiles[:, :], 0.0).then_inc(const_done, 1)
            dve.memset(src_t[:, COLS:COLS + RING_COLS], 0).then_inc(const_done, 1)
            dve.memset(end_row[:, TILES:TILES + TAIL_TILES], 0).then_inc(const_done, 1)
            dve.memset(incoming[:, :, :], LOWEST).then_inc(const_done, 1)
            dve.memset(carry[:, :], 0.0).then_inc(scan_done, 1)
            dve.memset(empty_row[:, :], LOWEST).then_inc(const_done, 1)
            dve.memset(no_hot[:, :], 0.0).then_inc(const_done, 1)
            dve.memset(prev_last[0:1, :], -1).then_inc(const_done, 1)
            dve.wait_ge(iota_done, 3)
            dve.tensor_copy(lane[:, :], lane_i[:, :]).then_inc(const_done, 1)
            dve.tensor_copy(lane_bf[:, :], lane_i[:, :]).then_inc(const_done, 1)
            dve.tensor_copy(part[:, :], part_i[:, :]).then_inc(const_done, 1)
            dve.wait_ge(const_done, 12)
            dve.tensor_scalar(ident[:, :], lane[:, :], part[:, 0:1], None, ALU.is_equal).then_inc(const_done, 1)
            dve.tensor_scalar(upper[:, :], lane[:, :], part[:, 0:1], None, ALU.is_ge).then_inc(const_done, 1)

            for s in range(TAIL_STEPS):
                dve.wait_ge(x_loaded[s], DMA)
                if s:
                    dve.wait_ge(var_done, TAIL_TILES * s)
                for k in range(TAIL_TILES):
                    dve.bn_stats(stats[:, k, :], x_all[:, s * TAIL_TILES + k, :]).then_inc(stats_done, 1)
                dve.wait_ge(stats_done, TAIL_TILES * (s + 1))
                for k in range(TAIL_TILES):
                    dve.bn_aggr(mean_var[:, s * TAIL_TILES + k, :], stats[:, k, :]).then_inc(var_done, 1)
                t = slice(s * TAIL_TILES, (s + 1) * TAIL_TILES)
                dve.wait_ge(std_done, s + 1)
                dve.reciprocal(rstd[:, t], std[:, t]).then_inc(norm_ready, 1)
                dve.wait_ge(norm_ready, 2 * s + 1)
                dve.scalar_tensor_tensor(out=shift[:, t], in0=mean_var[:, t, 0], scalar=-1.0,
                                         in1=rstd[:, t], op0=ALU.mult, op1=ALU.mult).then_inc(norm_ready, 1)

            dve.wait_ge(edges_loaded, 3 * DMA)
            dve.tensor_scalar(restart[:, :].bitcast(I32), dst_t[:, :], P - 1, None,
                              ALU.bitwise_and).then_inc(prep_done, 1)
            dve.wait_ge(prep_done, 1)
            dve.tensor_copy(dst_lane[:, :], restart[:, :].bitcast(I32)).then_inc(prep_done, 1)
            dve.wait_ge(prep_done, 2)
            dve.tensor_scalar(restart[:, :].bitcast(I32), dst_t[:, :], LANE_BITS, None,
                              ALU.arith_shift_right).then_inc(prep_done, 1)
            dve.wait_ge(prep_done, 3)
            dve.tensor_copy(dst_tile[:, :], restart[:, :].bitcast(I32)).then_inc(prep_done, 1)
            dve.tensor_copy(cols[:, 0:1], dst_t[:, 0:1]).then_inc(prep_done, 1)
            dve.wait_ge(prep_done, 5)
            dve.tensor_scalar(restart[:, :], dst_t[:, :], cols[:, 0:1], None, ALU.is_equal).then_inc(prep_done, 1)
            dve.tensor_tensor(cols[:, 2:3], dst_t[:, 0:1], prev_last[:, :], ALU.is_equal).then_inc(prep_done, 1)
            dve.wait_ge(prep_done, 7)
            dve.tensor_reduce(cols[:, 1:2], restart[:, :], AXIS.X, ALU.add).then_inc(prep_done, 1)
            dve.wait_ge(prep_done, 8)
            dve.tensor_scalar(cols[:, 4:5], cols[:, 1:2], part[:, 1:2], -1.0, ALU.add, ALU.add).then_inc(prep_done, 1)
            dve.scalar_tensor_tensor(out=cols[:, 3:4], in0=cols[:, 1:2], scalar=float(COLS),
                                     in1=cols[:, 2:3], op0=ALU.is_equal, op1=ALU.mult).then_inc(prep_done, 1)
            dve.tensor_tensor(restart[:, 1:COLS], dst_t[:, 1:COLS], dst_t[:, 0:COLS - 1],
                              ALU.not_equal).then_inc(prep_done, 1)
            dve.wait_ge(prep_done, 11)
            dve.tensor_copy(patch_row[:, :], cols[:, 4:5]).then_inc(prep_done, 1)
            dve.tensor_scalar(restart[:, 1:COLS], restart[:, 1:COLS], LOWEST, None, ALU.mult).then_inc(prep_done, 1)
            dve.memset(restart[:, 0:1], LOWEST).then_inc(prep_done, 1)
            dve.tensor_scalar(diag[:, 0, :], ident[:, :], cols[:, 2:3], None, ALU.mult).then_inc(join_diag, 1)
            dve.tensor_scalar(diag[:, 1, :], ident[:, :], cols[:, 3:4], None, ALU.mult).then_inc(join_diag, 1)
            dve.wait_ge(join_spread, 1)
            dve.tensor_scalar(join_row[:, :, :].rearrange("p a b -> p (a b)"), carry_ps[:, 0:2 * P],
                              -LOWEST, LOWEST, ALU.mult, ALU.add).then_inc(join_diag, 1)

            for l, (w, n) in enumerate(shapes):
                kc = w // P
                dve.wait_ge(const_done, CONSTS)
                if l:
                    dve.wait_ge(index_staged, STAGED * l)
                for b in range(BLOCKS):
                    dve.tensor_copy(index_stage[:, b, :], src_t[:, b * BLOCK_COLS:(b + 1) * BLOCK_COLS]
                                    ).then_inc(index_staged, 1)
                with dve.Fori(0, STEPS) as i:
                    for b in range(BLOCKS):
                        dve.wait_ge(landed[b], i * (DMA * BLOCK_COLS) + DMA * BLOCK_COLS * (STEPS * l + 1))
                        dve.wait_ge(edges_loaded, 3 * DMA)
                        dve.tensor_copy(
                            index_stage[:, b, :],
                            src_t[:, bass.ds(i * RING_COLS + (RING_COLS + b * BLOCK_COLS), BLOCK_COLS)],
                        ).then_inc(index_staged, 1)
                        if l == 0:
                            dve.wait_ge(hot_used[b], i + 1)
                        for u in range(BLOCK_COLS):
                            c = b * BLOCK_COLS + u
                            here = ring[:, c * w:(c + 1) * w]
                            before = ring[:, (c - 1) * w:c * w] if c else carry[:, 0:w]
                            dve.wait_ge(scan_done, i * SCANS_STEP + (SCANS * l + c + 1))
                            dve.scalar_tensor_tensor(
                                out=here, in0=before, scalar=restart[:, bass.ds(i * RING_COLS + c, 1)],
                                in1=here, op0=ALU.add, op1=ALU.max).then_inc(scan_done, 1)
                            if l == 0:
                                dve.tensor_scalar(hot[:, c, 0:P], lane_bf[:, :],
                                                  dst_lane[:, bass.ds(i * RING_COLS + c, 1)], None,
                                                  ALU.is_equal).then_inc(hot_ready, 1)
                                dve.tensor_scalar(hot[:, c, P:HOT], lane_bf[:, 0:TILES],
                                                  dst_tile[:, bass.ds(i * RING_COLS + c, 1)], None,
                                                  ALU.is_equal).then_inc(hot_ready, 1)
                    dve.wait_ge(scan_done, i * SCANS_STEP + (SCANS * l + RING_COLS + 1))
                    dve.tensor_copy(carry[:, 0:w], ring[:, (RING_COLS - 1) * w:RING_COLS * w]
                                    ).then_inc(scan_done, 1)

                if l == 0:
                    dve.wait_ge(count_ready, 1)
                    dve.tensor_copy(count[:, :], hist_ps[:, 0:TILES]).then_inc(ends_step, 1)
                    dve.wait_ge(count_spread, 1)
                    dve.tensor_copy(total[:, :], hist_ps[:, TILES:2 * TILES]).then_inc(ends_step, 1)
                    dve.wait_ge(ends_step, 2)
                    dve.tensor_tensor_scan(upto[:, :], total[:, :], zero_tiles[:, :], 0.0,
                                           ALU.add, ALU.add).then_inc(ends_step, 1)
                    dve.wait_ge(ends_step, 3)
                    dve.tensor_tensor(total[:, :], upto[:, :], total[:, :], ALU.subtract).then_inc(ends_step, 1)
                    dve.wait_ge(ends_step, 4)
                    dve.scalar_tensor_tensor(out=ends[:, :], in0=hist_ps[:, 0:TILES],
                                             scalar=-float(1 + P * COLS), in1=total[:, :],
                                             op0=ALU.add, op1=ALU.add).then_inc(ends_step, 1)
                    dve.wait_ge(ends_step, 5)
                    dve.scalar_tensor_tensor(out=upto[:, :], in0=count[:, :], scalar=0.0,
                                             in1=ends[:, :], op0=ALU.is_gt, op1=ALU.mult).then_inc(ends_step, 1)
                    dve.wait_ge(ends_step, 6)
                    dve.tensor_scalar(end_row[:, 0:TILES], upto[:, :], float(P * COLS), None,
                                      ALU.add).then_inc(ends_step, 1)

                dve.wait_ge(carry_turned, l + 1)
                dve.wait_ge(join_diag, 3)
                for c in range(kc):
                    dve.tensor_tensor_scan(carry_scan[:, c, :], join_row[:, 1, :],
                                           carry_ps[:, c * P:(c + 1) * P], 0.0,
                                           ALU.add, ALU.max).then_inc(join_step, 1)
                for c in range(kc):
                    before = sum(s[0] for s in shapes[:l]) // P
                    dve.wait_ge(join_step, before + c + 1)
                    dve.tensor_tensor(incoming[:, c, 1:P], carry_scan[:, c, 0:P - 1],
                                      join_row[:, 0, 1:P], ALU.add).then_inc(incoming_ready, 1)
                dve.wait_ge(incoming_turned, l + 1)
                dve.wait_ge(patch_landed, DMA * (l + 1))
                dve.tensor_tensor(patch[:, 0:w], patch[:, 0:w], back_ps[:, 0:w], ALU.max).then_inc(patched, 1)

                def stage_ends(half, first):
                    return dve.tensor_copy(end_stage[:, half, :], end_row[:, first]).then_inc(end_staged, 1)

                dve.wait_ge(ends_step, ENDS)
                if l:
                    dve.wait_ge(end_staged, 2 * (TAIL_STEPS + 1) * l)
                stage_ends(0, slice(0, HALF))
                stage_ends(1, slice(HALF, TAIL_TILES))

                def guard(i, k):
                    b = k % 2
                    dve.wait_ge(agg_turned, i * TAIL_TILES + (TILES * l + k + 1))
                    dve.tensor_scalar(finite[b][:, 0:w], turn_ps[b][:, 0:w].bitcast(I32), TOP_EXPONENT,
                                      TOP_EXPONENT, ALU.bitwise_and, ALU.bitwise_xor).then_inc(mask_done, 1)
                    dve.memset(agg[b][:, 0:w], 0.0).then_inc(mask_done, 1)
                    dve.wait_ge(mask_done, i * (2 * TAIL_TILES) + 2 * (TILES * l + k + 1))
                    dve.sem_inc(guard_open, 1)
                    dve.copy_predicated(agg[b][:, 0:w], finite[b][:, 0:w], turn_ps[b][:, 0:w]
                                        ).then_inc(agg_done, 1)

                def finish(i, k, first=False):
                    b, o = k % 2, k % OUT_RING
                    dve.wait_ge(z_ready, i * TAIL_TILES + (TILES * l + k + 1))
                    dve.tensor_tensor(z_sum[b][:, 0:n], mm_ps[b][:, 0:n],
                                      own[:, bass.ds(i * (TAIL_TILES * n) + k * n, n)],
                                      ALU.add).then_inc(sum_done, 1)
                    if not (first and k < OUT_RING):
                        dve.wait_ge(h_stored[o], i * (TAIL_TILES // OUT_RING * DMA)
                                    + (PER_OUT * l + k // OUT_RING * DMA))
                    dve.wait_ge(sum_done, i * TAIL_TILES + (TILES * l + k + 1))
                    made = dve.scalar_tensor_tensor(out=h_out[o][:, 0:n], in0=z_sum[b][:, 0:n],
                                                    scalar=SLOPE, in1=z_sum[b][:, 0:n],
                                                    op0=ALU.mult, op1=ALU.max)
                    if l < LAYERS - 1:
                        made.then_inc(h_done, 1)
                    else:
                        made.then_inc(act_done, 1)
                        dve.wait_ge(act_done, i * TAIL_TILES + (k + 1))
                        dve.tensor_tensor(h_out[o][:, 0:n], h_out[o][:, 0:n],
                                          own[:, bass.ds(i * (TAIL_TILES * n) + (TILES * n + k * n), n)],
                                          ALU.add).then_inc(h_done, 1)

                dve.wait_ge(own_done, TILES * (l + 1))
                if l == LAYERS - 1:
                    dve.wait_ge(residual_loaded, DMA)

                def tail(i, first):
                    for k in range(TAIL_TILES):
                        guard(i, k)
                        if k % HALF == HALF - 1:
                            dve.wait_ge(ends_step, ENDS)
                            stage_ends(k // HALF, bass.ds(i * TAIL_TILES + (TAIL_TILES + k + 1 - HALF), HALF))
                        if k:
                            finish(i, k - 1, first)
                    finish(i, TAIL_TILES - 1, first)

                if l == 0:
                    tail(0, True)
                with dve.Fori(1 if l == 0 else 0, TAIL_STEPS) as i:
                    tail(i, False)

        @block.tensor
        def _(pe):
            for b in range(BLOCKS):
                pe.sem_inc(hot_used[b], 1)
            pe.wait_ge(join_diag, 2)
            for f in range(2):
                mm = pe.matmul(carry_ps[:, f * P:(f + 1) * P], ones[:, :], diag[:, f, :],
                               start=True, stop=True)
            mm.then_inc(join_spread, 1)
            pe.wait_ge(weights_loaded, N_WEIGHTS)

            for l, (w, n) in enumerate(shapes):
                kc = w // P

                def own_pair(j):
                    for p in range(2):
                        pe.wait_ge(in_loaded[p], j * DMA + DMA * (PAIRS * l + 1))
                        for c in range(kc):
                            turn = pe.transpose(turn_ps[p][:, c * P:(c + 1) * P],
                                                h_in[p][:, c * P:(c + 1) * P], ident[:, :])
                        turn.then_inc(in_turned, 1)
                        pe.wait_ge(in_copied, j * 2 + (TILES * l + p + 1))
                        for c in range(kc):
                            pe.matmul(mm_ps[p][:, 0:n], h_turned[p][:, c, :], wr_sb[l][:, c, :],
                                      start=(c == 0), stop=False)
                        pe.matmul(mm_ps[p][:, 0:n], ones[0:1, :], b_sb[l][:, :],
                                  start=False, stop=True).then_inc(own_mm, 1)

                def histogram(i):
                    for b in range(BLOCKS):
                        pe.wait_ge(hot_ready, i * (2 * RING_COLS) + 2 * (b + 1) * BLOCK_COLS)
                        for u in range(BLOCK_COLS):
                            c = b * BLOCK_COLS + u
                            mm = pe.matmul(hist_ps[:, 0:TILES], hot[:, c, 0:P], hot[:, c, P:HOT],
                                           start=False, stop=False, skip_group_check=True)
                        mm.then_inc(hot_used[b], 1)

                if l == 0:
                    pe.wait_ge(const_done, CONSTS)
                    pe.matmul(hist_ps[:, 0:TILES], no_hot[:, 0:P], no_hot[:, P:HOT],
                              start=True, stop=False, skip_group_check=True)
                    with pe.Fori(0, PAIRS) as i:
                        histogram(i)
                        own_pair(i)
                    if STEPS > PAIRS:
                        with pe.Fori(PAIRS, STEPS) as i:
                            histogram(i)
                    pe.matmul(hist_ps[:, 0:TILES], no_hot[:, 0:P], no_hot[:, P:HOT],
                              start=False, stop=True, skip_group_check=True).then_inc(count_ready, 1)
                    pe.wait_ge(ends_step, 1)
                    pe.matmul(hist_ps[:, 0:TILES], upper[:, :], count[:, :], start=True, stop=True)
                    pe.matmul(hist_ps[:, TILES:2 * TILES], ones[:, :], count[:, :],
                              start=True, stop=True).then_inc(count_spread, 1)
                else:
                    with pe.Fori(0, PAIRS) as i:
                        own_pair(i)

                pe.wait_ge(scan_done, SCANS * (l + 1) + 1)
                for c in range(kc):
                    turn = pe.transpose(carry_ps[:, c * P:(c + 1) * P], carry[:, c * P:(c + 1) * P],
                                        ident[:, :])
                turn.then_inc(carry_turned, 1)
                pe.wait_ge(incoming_ready, sum(s[0] for s in shapes[:l + 1]) // P)
                for c in range(kc):
                    turn = pe.transpose(back_ps[:, c * P:(c + 1) * P], incoming[:, c, :], ident[:, :])
                turn.then_inc(incoming_turned, 1)

                def turn_agg(i, k):
                    pe.wait_ge(end_landed[k], i * DMA + DMA * (TAIL_STEPS * l + 1))
                    for c in range(kc):
                        turn = pe.transpose(turn_ps[k % 2][:, c * P:(c + 1) * P],
                                            ring[:, k * w + c * P:k * w + (c + 1) * P], ident[:, :])
                    turn.then_inc(agg_turned, 1)

                def project(i, k):
                    pe.wait_ge(agg_done, i * TAIL_TILES + (TILES * l + k + 1))
                    for c in range(kc):
                        mm = pe.matmul(mm_ps[k % 2][:, 0:n], agg[k % 2][:, c * P:(c + 1) * P],
                                       wl_sb[l][:, c, :], start=(c == 0), stop=(c == kc - 1))
                    mm.then_inc(z_ready, 1)

                pe.wait_ge(own_done, TILES * (l + 1))
                with pe.Fori(0, TAIL_STEPS) as i:
                    for k in range(TAIL_TILES):
                        turn_agg(i, k)
                        if k:
                            project(i, k - 1)
                    project(i, TAIL_TILES - 1)

        @block.scalar
        def _(act):
            for l, (wl, bl, wr) in enumerate(weights):
                act.dma_start(wr_sb[l][:, :, :], wr.rearrange("(c p) n -> p c n", p=P)).then_inc(weights_loaded, DMA)
                act.dma_start(wl_sb[l][:, :, :], wl.rearrange("(c p) n -> p c n", p=P)).then_inc(weights_loaded, DMA)
                act.dma_start(b_sb[l][:, :], bl.rearrange("(a n) -> a n", a=1)).then_inc(weights_loaded, DMA)
            act.wait_ge(const_done, CONSTS)
            for s in range(TAIL_STEPS):
                t = slice(s * TAIL_TILES, (s + 1) * TAIL_TILES)
                act.wait_ge(var_done, TAIL_TILES * (s + 1))
                nc.scalar.activation(std[:, t], mean_var[:, t, 1], ACT.Sqrt, bias=eps[:, 0:1]).then_inc(std_done, 1)
                act.wait_ge(norm_ready, 2 * (s + 1))
                for k in range(s * TAIL_TILES, (s + 1) * TAIL_TILES):
                    nc.scalar.activation(h0_all[:, k, :], x_all[:, k, :], ACT.Relu, bias=shift[:, k:k + 1],
                                         scale=rstd[:, k:k + 1]).then_inc(h0_done, 1)

            for l, (w, n) in enumerate(shapes):
                if l == 0:
                    act.wait_ge(h0_stored, DMA * TAIL_STEPS)
                else:
                    for b in range(OUT_RING):
                        act.wait_ge(h_stored[b], PER_OUT * l)
                if l == LAYERS - 1:
                    act.dma_start(own[:, TILES * n:TILES * (n + F_IN)].rearrange("p (t f) -> p t f", f=F_IN),
                                  x.rearrange("(t p) f -> p t f", p=P)).then_inc(residual_loaded, DMA)

                def load(tile, p):
                    act.dma_start(h_in[p][:, 0:w], tables[l][bass.ds(tile * P, P), :]).then_inc(in_loaded[p], DMA)

                def copy_pair(j, more):
                    for p in range(2):
                        act.wait_ge(in_turned, j * 2 + (TILES * l + p + 1))
                        nc.scalar.activation(h_turned[p][:, :, :].rearrange("p c m -> p (c m)")[:, 0:w],
                                             turn_ps[p][:, 0:w], ACT.Copy).then_inc(in_copied, 1)
                        if more:
                            load(j * 2 + (p + 2), p)
                        act.wait_ge(own_mm, j * 2 + (TILES * l + p + 1))
                        act.wait_ge(weights_loaded, N_WEIGHTS)
                        nc.scalar.activation(own[:, bass.ds(j * (2 * n) + p * n, n)], mm_ps[p][:, 0:n],
                                             ACT.Copy).then_inc(own_done, 1)

                load(0, 0)
                load(1, 1)
                with act.Fori(0, PAIRS - 1) as j:
                    copy_pair(j, True)
                copy_pair(PAIRS - 1, False)

        @block.sync
        def _(sp):
            x_rows = x.rearrange("(t p) f -> p t f", p=P)
            h0_rows = tables[0].rearrange("(t p) f -> p t f", p=P)
            for s in range(TAIL_STEPS):
                t = slice(s * TAIL_TILES, (s + 1) * TAIL_TILES)
                sp.dma_start(x_all[:, t, :], x_rows[:, t, :]).then_inc(x_loaded[s], DMA)
            sp.dma_start(dst_t[:, :], dst).then_inc(edges_loaded, DMA)
            sp.dma_start(src_t[:, 0:COLS], src).then_inc(edges_loaded, DMA)
            sp.wait_ge(const_done, CONSTS)
            with nc.allow_non_contiguous_dma(reason="one word of each partition's run of edges"):
                sp.dma_start(prev_last[1:P, :], dst[0:P - 1, COLS - 1:COLS]).then_inc(edges_loaded, DMA)
            for w in widths:
                sp.dma_start(logs[w][P * COLS:LOG_ROWS, :], empty_row[:, 0:w]).then_inc(empty_stored, DMA)
            for s in range(TAIL_STEPS):
                t = slice(s * TAIL_TILES, (s + 1) * TAIL_TILES)
                sp.wait_ge(h0_done, TAIL_TILES * (s + 1))
                sp.dma_start(h0_rows[:, t, :], h0_all[:, t, :]).then_inc(h0_stored, DMA)

            for l, (w, n) in enumerate(shapes):
                with sp.Fori(0, STEPS) as i:
                    for b in range(BLOCKS):
                        sp.wait_ge(scan_done, i * SCANS_STEP + (SCANS * l + (b + 1) * BLOCK_COLS + 2))
                        c = b * BLOCK_COLS
                        sp.dma_start(log_block(l, i, b), ring[:, c * w:(c + BLOCK_COLS) * w]).then_inc(logged[b], DMA)
                made = tables[l + 1] if l < LAYERS - 1 else out
                with sp.Fori(0, TAIL_STEPS) as i:
                    for k in range(TAIL_TILES):
                        sp.wait_ge(h_done, i * TAIL_TILES + (TILES * l + k + 1))
                        sp.dma_start(made[bass.ds(i * (TAIL_TILES * P) + k * P, P), :],
                                     h_out[k % OUT_RING][:, 0:n]).then_inc(h_stored[k % OUT_RING], DMA)
            for b in range(OUT_RING):
                sp.wait_ge(h_stored[b], PER_OUT * LAYERS)


def kernel(**inputs):
    import numpy as np
    import concourse.bacc as bacc
    from concourse.bass_utils import run_bass_kernel_spmd

    x = np.ascontiguousarray(inputs["x"])
    nodes, features = x.shape
    edges = inputs["src"].shape[0]
    group = P * TAIL_TILES
    rows = -(-nodes // group) * group
    cols = -(-edges // (P * RING_COLS)) * RING_COLS

    def filled(a, size, fill):
        whole = np.full(size, fill, a.dtype)
        whole[:a.shape[0]] = a
        return whole.reshape(P, -1)

    x_rows = np.zeros((rows, features), x.dtype)
    x_rows[:nodes] = x
    arrays = {
        "x": x_rows,
        "src": filled(np.asarray(inputs["src"]), P * cols, 0),
        "dst": filled(np.asarray(inputs["dst"]), P * cols, NO_NODE),
    }
    layers = [f"L0_gnn_{part}{l}" for l in (1, 2, 3) for part in ("Wl", "bl", "Wr")]
    for name in layers:
        arrays[name] = np.ascontiguousarray(inputs[name])
    nc = bacc.Bacc("TRN2", target_bir_lowering=False, num_devices=1)
    given = {
        name: nc.dram_tensor(name, a.shape, mybir.dt.from_np(a.dtype), kind="ExternalInput").ap()
        for name, a in arrays.items()
    }
    out = nc.dram_tensor("out", (rows, arrays["L0_gnn_Wl3"].shape[1]), F32, kind="ExternalOutput").ap()
    weights = [tuple(given[name] for name in layers[3 * l:3 * l + 3]) for l in range(3)]
    gnn_program(nc, given["x"], given["src"], given["dst"], weights, out)
    r = run_bass_kernel_spmd(nc, [arrays], core_ids=[0])
    return r.results[0]["out"][:nodes]
```

```python
from contextlib import ExitStack

import concourse.bass as bass
from concourse import mybir

ALU = mybir.AluOpType
ACT = mybir.ActivationFunctionType
AXIS = mybir.AxisListType
F32 = mybir.dt.float32
BF16 = mybir.dt.bfloat16
I32 = mybir.dt.int32
U32 = mybir.dt.uint32

P = 128
LANE_BITS = 7
BLOCKS = 9
BLOCK_COLS = 6
RING_COLS = BLOCKS * BLOCK_COLS
TAIL_TILES = 10
TAIL_PAIRS = TAIL_TILES // 2
SHARES = (0, 4, TAIL_TILES)
BUFFERS = (0, 1, 0, 1, 2)
REUSE = tuple(next(d for d in range(1, TAIL_PAIRS + 1) if BUFFERS[q - d] == BUFFERS[q])
              for q in range(TAIL_PAIRS))
ACT_TILES = 7
DMA = 16
LOWEST = -3.4028234663852886e38
TOP_EXPONENT = 0x7F000000
SLOPE = 0.01
EPS = 1e-5
NO_NODE = 1 << 20


def gnn_program(nc, x, src, dst, weights, out):
    NODES, F_IN = x.shape
    COLS = src.shape[1]
    TILES = NODES // P
    STEPS = COLS // RING_COLS
    TAIL_STEPS = TILES // TAIL_TILES
    PAIRS = TILES // 2
    assert COLS % RING_COLS == 0 and TILES % TAIL_TILES == 0
    assert PAIRS <= STEPS
    shapes = [wl.shape for wl, _, _ in weights]
    F_MAX = max(max(s) for s in shapes)
    KC_MAX = F_MAX // P
    LOG_ROWS = P * COLS + 1
    SCANS_STEP = RING_COLS + 1
    SCANS = STEPS * SCANS_STEP
    STAGED = STEPS * BLOCKS + BLOCKS

    tables = [nc.dram_tensor(f"features_{l}", (NODES, s[0]), F32).ap() for l, s in enumerate(shapes)]
    widths = sorted({s[0] for s in shapes})
    logs = {w: nc.dram_tensor(f"running_max_log_{w}", (LOG_ROWS, w), F32).ap() for w in widths}

    with ExitStack() as ctx:
        def sb(name, shape, dt=F32):
            return ctx.enter_context(nc.sbuf_tensor(name, shape, dt))

        def ps(name, shape, dt=F32):
            return ctx.enter_context(nc.psum_tensor(name, shape, dt))

        def sem(name):
            return ctx.enter_context(nc.semaphore(name))

        ring = sb("ring", [P, RING_COLS * F_MAX])
        second = RING_COLS * F_IN
        x_all = ring[:, 0:TILES * F_IN].rearrange("p (t f) -> p t f", f=F_IN)
        h0_all = ring[:, second:second + TILES * F_IN].rearrange("p (t f) -> p t f", f=F_IN)
        HOT = P + TILES
        HOT_WORDS = RING_COLS * HOT // 2
        assert second >= TILES * F_IN and second + max(TILES * F_IN, HOT_WORDS) <= RING_COLS * F_MAX
        hot = ring[:, second:second + HOT_WORDS].bitcast(BF16).rearrange("p (c h) -> p c h", h=HOT)

        own = sb("own", [P, TILES * F_MAX])
        src_t = sb("src_t", [P, COLS + RING_COLS], I32)
        dst_t = sb("dst_t", [P, COLS], I32)
        restart = sb("restart", [P, COLS])
        dst_lane = sb("dst_lane", [P, COLS], BF16)
        dst_tile = sb("dst_tile", [P, COLS], BF16)
        index_stage = sb("index_stage", [P, BLOCKS, BLOCK_COLS], I32)
        end_row = sb("end_row", [P, TILES + TAIL_TILES], I32)
        end_stage = [sb(f"end_stage{h}", [P, SHARES[h + 1] - SHARES[h]], I32) for h in range(2)]
        wl_sb, wr_sb, b_sb = [], [], []
        for l, (k, n) in enumerate(shapes):
            wl_sb.append(sb(f"wl{l}", [P, k // P, n]))
            wr_sb.append(sb(f"wr{l}", [P, k // P, n]))
            b_sb.append(sb(f"b{l}", [1, n]))
        lane_i = sb("lane_i", [P, P], I32)
        lane = sb("lane", [P, P])
        lane_bf = sb("lane_bf", [P, P], BF16)
        part_i = sb("part_i", [P, 2], I32)
        part = sb("part", [P, 2])
        ident = sb("ident", [P, P])
        upper = sb("upper", [P, P])
        ones = sb("ones", [P, P])
        prev_last = sb("prev_last", [P, 1], I32)
        cols = sb("cols", [P, 8])
        patch_row = sb("patch_row", [P, 1], I32)
        diag = sb("diag", [P, 2, P])
        join_row = sb("join_row", [P, 2, P])
        stats = sb("stats", [P, TAIL_TILES, 6])
        mean_var = sb("mean_var", [P, TILES, 2])
        std = sb("std", [P, TILES])
        rstd = sb("rstd", [P, TILES])
        shift = sb("shift", [P, TILES])
        eps = sb("eps", [P, 1])
        unsorted = sb("unsorted", [P, 1], I32)
        count = sb("count", [P, TILES])
        total = sb("total", [P, TILES])
        zeros = sb("zeros", [P, 2 * F_MAX])
        empty_row = sb("empty_row", [1, F_MAX])
        no_hot = sb("no_hot", [P, HOT], BF16)
        upto = sb("upto", [P, TILES])
        ends = sb("ends", [P, TILES])
        zero_tiles = sb("zero_tiles", [P, TILES])
        h_in = [sb(f"h_in{b}", [P, F_MAX]) for b in range(2)]
        h_turned = [sb(f"h_turned{b}", [P, KC_MAX, P]) for b in range(2)]
        agg = [sb(f"agg{b}", [P, 2 * F_MAX]) for b in range(3)]
        finite = [sb(f"finite{b}", [P, 2 * F_MAX], I32) for b in range(3)]
        z_sum = [sb(f"z_sum{b}", [P, 2 * F_MAX]) for b in range(3)]
        h_out = [sb(f"h_out{k}", [P, 2 * F_MAX]) for k in range(TAIL_PAIRS)]
        carry = sb("carry", [P, F_MAX])
        carry_scan = sb("carry_scan", [P, KC_MAX, P])
        incoming = sb("incoming", [P, KC_MAX, P])
        patch = sb("patch", [P, F_MAX])

        turn_ps = [ps(f"turn_ps{b}", [P, 512]) for b in range(3)]
        mm_ps = [ps(f"mm_ps{b}", [P, 512]) for b in range(3)]
        hist_ps = mm_ps[2]
        carry_ps = ps("carry_ps", [P, 512])
        back_ps = ps("back_ps", [P, 512])

        x_loaded = [sem(f"x_loaded{s}") for s in range(TAIL_STEPS)]
        edges_loaded, weights_loaded = sem("edges_loaded"), sem("weights_loaded")
        iota_done, const_done, prep_done = sem("iota_done"), sem("const_done"), sem("prep_done")
        stats_done, var_done, std_done, norm_ready = (
            sem("stats_done"), sem("var_done"), sem("std_done"), sem("norm_ready"))
        h0_scaled, h0_rest_done = sem("h0_scaled"), sem("h0_rest_done")
        h0_done, h0_stored, empty_stored = sem("h0_done"), sem("h0_stored"), sem("empty_stored")
        join_diag, join_spread = sem("join_diag"), sem("join_spread")
        index_staged, gathers_open = sem("index_staged"), sem("gathers_open")
        landed = [sem(f"landed{b}") for b in range(BLOCKS)]
        scan_done = sem("scan_done")
        logged = [sem(f"logged{b}") for b in range(BLOCKS)]
        hot_ready, hot_used = sem("hot_ready"), [sem(f"hot_used{b}") for b in range(BLOCKS)]
        count_ready, count_spread, ends_step = sem("count_ready"), sem("count_spread"), sem("ends_step")
        in_loaded = [sem(f"in_loaded{b}") for b in range(2)]
        in_turned, in_copied, own_mm, own_done = (
            sem("in_turned"), sem("in_copied"), sem("own_mm"), sem("own_done"))
        carry_turned, join_step, incoming_ready, incoming_turned = (
            sem("carry_turned"), sem("join_step"), sem("incoming_ready"), sem("incoming_turned"))
        patch_landed, patched, patch_stored = sem("patch_landed"), sem("patched"), sem("patch_stored")
        end_staged = sem("end_staged")
        end_landed = [sem(f"end_landed{k}") for k in range(TAIL_TILES)]
        agg_turned, mask_done, guard_open, agg_done = (
            sem("agg_turned"), sem("mask_done"), sem("guard_open"), sem("agg_done"))
        z_ready, sum_done, act_done, h_done = (
            sem("z_ready"), sem("sum_done"), sem("act_done"), sem("h_done"))
        agg_zeroed = sem("agg_zeroed")
        h_stored = [sem(f"h_stored{k}") for k in range(TAIL_PAIRS)]
        residual_loaded = sem("residual_loaded")

        BINS = NODES + 1
        SLOTS = BINS + P
        next_row = nc.dram_tensor("sort_next_row", (SLOTS, 1), F32).ap()
        sorted_src = nc.dram_tensor("sorted_src", (P * COLS, 1), I32).ap()
        sorted_dst = nc.dram_tensor("sorted_dst", (P * COLS, 1), I32).ap()
        assert 2 * SLOTS <= RING_COLS * F_MAX
        bin_counts, bin_starts = ring[0:1, 0:SLOTS], ring[0:1, SLOTS:2 * SLOTS]
        s_dst_row = ring[:, 0:P].bitcast(I32)
        s_key_row, s_equal, s_prior = ring[:, P:2 * P], ring[:, 2 * P:3 * P], ring[:, 3 * P:4 * P]
        s_int = ring[:, 4 * P:4 * P + 8].bitcast(I32)
        s_f = ring[:, 4 * P + 8:4 * P + 16]
        order_checked, order_summed, unsorted_known = (
            sem("order_checked"), sem("order_summed"), sem("unsorted_known"))
        sort_free, sort_loaded, sort_keyed, sort_fetched = (
            sem("sort_free"), sem("sort_loaded"), sem("sort_keyed"), sem("sort_fetched"))
        sort_placed, sort_put, sort_v, sort_open = (
            sem("sort_placed"), sem("sort_put"), sem("sort_v"), sem("sort_open"))
        sort_bins, sort_done = sem("sort_bins"), sem("sort_done")
        sort_w, sort_x = sem("sort_w"), sem("sort_x")

        LAYERS = len(shapes)
        CONSTS = 15
        PREP = 14
        ENDS = 7
        N_WEIGHTS = 3 * LAYERS * DMA
        PER_OUT = TAIL_STEPS * DMA

        def log_block(l, step, b):
            w = shapes[l][0]
            body = logs[w][0:P * COLS, :].rearrange("(p c) f -> p (c f)", p=P)
            return body[:, bass.ds((step * BLOCKS + b) * (BLOCK_COLS * w), BLOCK_COLS * w)]

        block = ctx.enter_context(nc.Block())

        @block.gpsimd
        def _(pool):
            pool.iota(lane_i[:, :], [[1, P]], base=0, channel_multiplier=0).then_inc(iota_done, 1)
            pool.iota(part_i[:, 0:1], [[0, 1]], base=0, channel_multiplier=1).then_inc(iota_done, 1)
            pool.iota(part_i[:, 1:2], [[0, 1]], base=0, channel_multiplier=COLS).then_inc(iota_done, 1)

            def sort_group(g, place):
                n = g + COLS if place else g
                pool.wait_ge(sort_free, n + 1)
                flat = dst.rearrange("p c -> (p c)")
                pool.dma_start(s_dst_row, flat[bass.ds(g * P, P)].partition_broadcast(P)
                               ).then_inc(sort_loaded, DMA)
                with nc.allow_non_contiguous_dma(reason="one edge in each partition"):
                    pool.dma_start(s_int[:, 0:1], flat[bass.ds(g * P, P)].rearrange("(p a) -> p a", a=1)
                                   ).then_inc(sort_loaded, DMA)
                    pool.dma_start(s_int[:, 1:2], src.rearrange("p c -> (p c)")[bass.ds(g * P, P)]
                                   .rearrange("(p a) -> p a", a=1)).then_inc(sort_loaded, DMA)
                pool.wait_ge(sort_keyed, n + 1)
                pool.sem_inc(sort_open, 1)
                pool.indirect_dma_start(s_f[:, 1:2], None, next_row,
                                        bass.IndirectOffsetOnAxis(ap=s_int[:, 2:3].bitcast(U32), axis=0)
                                        ).then_inc(sort_fetched, DMA)
                pool.wait_ge(sort_placed, n + 1)
                pool.sem_inc(sort_open, 1)
                pool.indirect_dma_start(next_row,
                                        bass.IndirectOffsetOnAxis(ap=s_int[:, 3:4].bitcast(U32), axis=0),
                                        s_f[:, 4:5], None).then_inc(sort_put, DMA)
                if place:
                    for what, to in ((s_int[:, 1:2], sorted_src), (s_int[:, 0:1], sorted_dst)):
                        pool.indirect_dma_start(to, bass.IndirectOffsetOnAxis(
                            ap=s_int[:, 4:5].bitcast(U32), axis=0), what, None).then_inc(sort_put, DMA)
                pool.wait_ge(sort_put, g * (3 * DMA) + DMA * (COLS + 3) if place else g * DMA + DMA)
                pool.sem_inc(sort_open, 1)

            pool.wait_ge(unsorted_known, 1)
            with pool.If(pool.value_load(unsorted[0:1, 0:1], min_val=0, max_val=1 << 24)):
                next_flat = next_row.rearrange("s a -> a s")
                pool.wait_ge(sort_bins, 1)
                pool.dma_start(next_flat, bin_counts).then_inc(sort_done, DMA)
                pool.wait_ge(sort_done, DMA)
                with pool.Fori(0, COLS) as g:
                    sort_group(g, False)
                pool.wait_ge(sort_free, COLS + 1)
                pool.dma_start(bin_counts, next_flat).then_inc(sort_done, DMA)
                pool.wait_ge(sort_bins, 3)
                pool.dma_start(next_flat, bin_starts).then_inc(sort_done, DMA)
                pool.wait_ge(sort_done, 3 * DMA)
                with pool.Fori(0, COLS) as g:
                    sort_group(g, True)
                in_runs = sorted_dst.rearrange("(p c) a -> p (c a)", p=P)
                pool.dma_start(dst_t[:, :], in_runs).then_inc(sort_done, DMA)
                pool.dma_start(src_t[:, 0:COLS], sorted_src.rearrange("(p c) a -> p (c a)", p=P)
                               ).then_inc(sort_done, DMA)
                with nc.allow_non_contiguous_dma(reason="one word of each partition's run of edges"):
                    pool.dma_start(prev_last[1:P, :], in_runs[0:P - 1, COLS - 1:COLS]).then_inc(sort_done, DMA)
                pool.wait_ge(sort_done, 6 * DMA)

            for l, (w, _n) in enumerate(shapes):
                if l == 0:
                    pool.wait_ge(h0_stored, DMA * TAIL_STEPS)
                else:
                    for b in range(TAIL_PAIRS):
                        pool.wait_ge(h_stored[b], PER_OUT * l)
                def gather(i, first):
                    for b in range(BLOCKS):
                        pool.wait_ge(index_staged, i * BLOCKS + (STAGED * l + b + 1))
                        if not first:
                            pool.wait_ge(logged[b], i * DMA + DMA * STEPS * l)
                        pool.sem_inc(gathers_open, 1)
                        for u in range(BLOCK_COLS):
                            c = b * BLOCK_COLS + u
                            pool.indirect_dma_start(
                                ring[:, c * w:(c + 1) * w], None, tables[l],
                                bass.IndirectOffsetOnAxis(
                                    ap=index_stage[:, b, u:u + 1].bitcast(U32), axis=0),
                            ).then_inc(landed[b], DMA)

                if l == 0:
                    gather(0, True)
                with pool.Fori(1 if l == 0 else 0, STEPS) as i:
                    gather(i, False)
                for b in range(BLOCKS):
                    pool.wait_ge(logged[b], DMA * STEPS * (l + 1))
                pool.wait_ge(prep_done, PREP)
                pool.indirect_dma_start(
                    patch[:, 0:w], None, logs[w],
                    bass.IndirectOffsetOnAxis(ap=patch_row[:, 0:1].bitcast(U32), axis=0),
                ).then_inc(patch_landed, DMA)
                pool.wait_ge(patched, l + 1)
                pool.indirect_dma_start(
                    logs[w], bass.IndirectOffsetOnAxis(ap=patch_row[:, 0:1].bitcast(U32), axis=0),
                    patch[:, 0:w], None,
                ).then_inc(patch_stored, DMA)
                pool.wait_ge(patch_stored, DMA * (l + 1))
                pool.wait_ge(empty_stored, DMA * len(widths))
                with pool.Fori(0, TAIL_STEPS) as i:
                    for k in range(TAIL_TILES):
                        h = int(k >= SHARES[1])
                        if k in SHARES:
                            pool.wait_ge(end_staged, i * 2 + (2 * (TAIL_STEPS + 1) * l + h + 1))
                            pool.sem_inc(gathers_open, 1)
                        pool.indirect_dma_start(
                            ring[:, k * w:(k + 1) * w], None, logs[w],
                            bass.IndirectOffsetOnAxis(
                                ap=end_stage[h][:, k - SHARES[h]:k - SHARES[h] + 1].bitcast(U32), axis=0),
                        ).then_inc(end_landed[k], DMA)

        @block.vector
        def _(dve):
            dve.memset(ones[:, :], 1.0).then_inc(const_done, 1)
            dve.memset(eps[:, :], EPS).then_inc(const_done, 1)
            dve.memset(zero_tiles[:, :], 0.0).then_inc(const_done, 1)
            dve.memset(src_t[:, COLS:COLS + RING_COLS], 0).then_inc(const_done, 1)
            dve.memset(end_row[:, TILES:TILES + TAIL_TILES], 0).then_inc(const_done, 1)
            dve.memset(incoming[:, :, :], LOWEST).then_inc(const_done, 1)
            dve.memset(carry[:, :], 0.0).then_inc(scan_done, 1)
            dve.memset(empty_row[:, :], LOWEST).then_inc(const_done, 1)
            dve.memset(no_hot[:, :], 0.0).then_inc(const_done, 1)
            dve.memset(zeros[:, :], 0.0).then_inc(const_done, 1)
            dve.memset(prev_last[0:1, :], -1).then_inc(const_done, 1)
            dve.wait_ge(iota_done, 3)
            dve.tensor_copy(lane[:, :], lane_i[:, :]).then_inc(const_done, 1)
            dve.tensor_copy(lane_bf[:, :], lane_i[:, :]).then_inc(const_done, 1)
            dve.tensor_copy(part[:, :], part_i[:, :]).then_inc(const_done, 1)
            dve.wait_ge(const_done, 13)
            dve.tensor_scalar(ident[:, :], lane[:, :], part[:, 0:1], None, ALU.is_equal).then_inc(const_done, 1)
            dve.tensor_scalar(upper[:, :], lane[:, :], part[:, 0:1], None, ALU.is_ge).then_inc(const_done, 1)

            def statistics(s):
                dve.wait_ge(x_loaded[s], DMA)
                if s:
                    dve.wait_ge(var_done, TAIL_TILES * s)
                for k in range(TAIL_TILES):
                    dve.bn_stats(stats[:, k, :], x_all[:, s * TAIL_TILES + k, :]).then_inc(stats_done, 1)
                dve.wait_ge(stats_done, TAIL_TILES * (s + 1))
                for k in range(TAIL_TILES):
                    dve.bn_aggr(mean_var[:, s * TAIL_TILES + k, :], stats[:, k, :]).then_inc(var_done, 1)

            def normalise(s):
                t = slice(s * TAIL_TILES, (s + 1) * TAIL_TILES)
                dve.wait_ge(std_done, s + 1)
                dve.reciprocal(rstd[:, t], std[:, t]).then_inc(norm_ready, 1)
                dve.wait_ge(norm_ready, 2 * s + 1)
                dve.scalar_tensor_tensor(out=shift[:, t], in0=mean_var[:, t, 0], scalar=-1.0,
                                         in1=rstd[:, t], op0=ALU.mult, op1=ALU.mult).then_inc(norm_ready, 1)
                own_share = slice(s * TAIL_TILES + ACT_TILES, (s + 1) * TAIL_TILES)
                dve.wait_ge(norm_ready, 2 * s + 2)
                for k in range(own_share.start, own_share.stop):
                    dve.tensor_scalar(h0_all[:, k, :], x_all[:, k, :], rstd[:, k:k + 1], shift[:, k:k + 1],
                                      ALU.mult, ALU.add).then_inc(h0_scaled, 1)
                dve.wait_ge(h0_scaled, (TAIL_TILES - ACT_TILES) * (s + 1))
                dve.tensor_scalar(h0_all[:, own_share, :], h0_all[:, own_share, :], 0.0, None,
                                  ALU.max).then_inc(h0_rest_done, 1)

            for s in range(TAIL_STEPS):
                statistics(s)
                if s:
                    normalise(s - 1)
            dve.wait_ge(edges_loaded, 3 * DMA)
            dve.tensor_tensor(restart[:, 1:COLS], dst_t[:, 1:COLS], dst_t[:, 0:COLS - 1],
                              ALU.is_lt).then_inc(order_checked, 1)
            dve.tensor_tensor(restart[:, 0:1], dst_t[:, 0:1], prev_last[:, :], ALU.is_lt).then_inc(order_checked, 1)
            dve.wait_ge(order_checked, 2)
            dve.tensor_reduce(cols[:, 5:6], restart[:, :], AXIS.X, ALU.add).then_inc(order_checked, 1)
            normalise(TAIL_STEPS - 1)

            def sort_group(g, place):
                n = g + COLS if place else g
                done = 5
                dve.wait_ge(sort_loaded, n * (3 * DMA) + 3 * DMA)
                dve.tensor_scalar(s_key_row, s_dst_row, float(NODES), None, ALU.min).then_inc(sort_v, 1)
                dve.tensor_scalar(s_f[:, 0:1], s_int[:, 0:1], float(NODES), None, ALU.min).then_inc(sort_v, 1)
                dve.wait_ge(sort_v, n * done + 2)
                dve.tensor_copy(s_int[:, 2:3], s_f[:, 0:1]).then_inc(sort_keyed, 1)
                dve.tensor_scalar(s_equal, s_key_row, s_f[:, 0:1], None, ALU.is_equal).then_inc(sort_v, 1)
                dve.wait_ge(sort_v, n * done + 3)
                dve.scalar_tensor_tensor(out=s_prior, in0=lane[:, :], scalar=part[:, 0:1], in1=s_equal,
                                         op0=ALU.is_lt, op1=ALU.mult).then_inc(sort_v, 1)
                dve.tensor_reduce(s_f[:, 3:4], s_equal, AXIS.X, ALU.add).then_inc(sort_v, 1)
                dve.wait_ge(sort_v, n * done + 5)
                dve.tensor_reduce(s_f[:, 2:3], s_prior, AXIS.X, ALU.add).then_inc(sort_w, 1)
                dve.wait_ge(sort_w, n * 4 + 1)
                dve.wait_ge(sort_fetched, n * DMA + DMA)
                dve.tensor_tensor(s_f[:, 4:5], s_f[:, 1:2], s_f[:, 3:4], ALU.add).then_inc(sort_w, 1)
                dve.tensor_tensor(s_int[:, 4:5], s_f[:, 1:2], s_f[:, 2:3], ALU.add).then_inc(sort_w, 1)
                dve.scalar_tensor_tensor(out=s_f[:, 5:6], in0=s_f[:, 2:3], scalar=1.0, in1=s_f[:, 3:4],
                                         op0=ALU.add, op1=ALU.is_equal).then_inc(sort_w, 1)
                dve.wait_ge(sort_w, n * 4 + 4)
                dve.tensor_scalar(s_f[:, 6:7], part[:, 0:1], float(BINS), None, ALU.add).then_inc(sort_x, 1)
                dve.wait_ge(sort_x, n * 3 + 1)
                dve.tensor_tensor(s_f[:, 7:8], s_f[:, 0:1], s_f[:, 6:7], ALU.subtract).then_inc(sort_x, 1)
                dve.wait_ge(sort_x, n * 3 + 2)
                dve.tensor_tensor(s_f[:, 7:8], s_f[:, 7:8], s_f[:, 5:6], ALU.mult).then_inc(sort_x, 1)
                dve.wait_ge(sort_x, n * 3 + 3)
                dve.tensor_tensor(s_int[:, 3:4], s_f[:, 7:8], s_f[:, 6:7], ALU.add).then_inc(sort_placed, 1)
                dve.wait_ge(sort_put, g * (3 * DMA) + DMA * (COLS + 3) if place else g * DMA + DMA)
                dve.sem_inc(sort_free, 1)

            dve.wait_ge(order_summed, 1)
            dve.tensor_copy(unsorted[:, :], back_ps[:, 0:1]).then_inc(unsorted_known, 1)
            dve.wait_ge(unsorted_known, 1)
            with dve.If(dve.value_load(unsorted[0:1, 0:1], min_val=0, max_val=1 << 24)):
                dve.wait_ge(h0_stored, DMA * TAIL_STEPS)
                dve.memset(bin_counts, 0.0).then_inc(sort_bins, 1)
                dve.wait_ge(sort_done, DMA)
                dve.sem_inc(sort_free, 1)
                with dve.Fori(0, COLS) as g:
                    sort_group(g, False)
                dve.wait_ge(sort_done, 2 * DMA)
                dve.memset(bin_starts[:, 0:1], 0.0).then_inc(sort_bins, 1)
                dve.tensor_tensor_scan(bin_starts[:, 1:SLOTS], bin_counts[:, 0:SLOTS - 1],
                                       bin_counts[:, 0:SLOTS - 1], 0.0, ALU.add, ALU.max
                                       ).then_inc(sort_bins, 1)
                dve.wait_ge(sort_done, 3 * DMA)
                with dve.Fori(0, COLS) as g:
                    sort_group(g, True)
                dve.wait_ge(sort_done, 6 * DMA)

            def stage_first_step():
                for b in range(BLOCKS):
                    dve.tensor_copy(index_stage[:, b, :], src_t[:, b * BLOCK_COLS:(b + 1) * BLOCK_COLS]
                                    ).then_inc(index_staged, 1)

            stage_first_step()

            dve.tensor_scalar(restart[:, :].bitcast(I32), dst_t[:, :], P - 1, None,
                              ALU.bitwise_and).then_inc(prep_done, 1)
            dve.wait_ge(prep_done, 1)
            dve.tensor_copy(dst_lane[:, :], restart[:, :].bitcast(I32)).then_inc(prep_done, 1)
            dve.wait_ge(prep_done, 2)
            dve.tensor_scalar(restart[:, :].bitcast(I32), dst_t[:, :], LANE_BITS, None,
                              ALU.arith_shift_right).then_inc(prep_done, 1)
            dve.wait_ge(prep_done, 3)
            dve.tensor_copy(dst_tile[:, :], restart[:, :].bitcast(I32)).then_inc(prep_done, 1)
            dve.tensor_copy(cols[:, 0:1], dst_t[:, 0:1]).then_inc(prep_done, 1)
            dve.wait_ge(prep_done, 5)
            dve.tensor_scalar(restart[:, :], dst_t[:, :], cols[:, 0:1], None, ALU.is_equal).then_inc(prep_done, 1)
            dve.tensor_tensor(cols[:, 2:3], dst_t[:, 0:1], prev_last[:, :], ALU.is_equal).then_inc(prep_done, 1)
            dve.wait_ge(prep_done, 7)
            dve.tensor_reduce(cols[:, 1:2], restart[:, :], AXIS.X, ALU.add).then_inc(prep_done, 1)
            dve.wait_ge(prep_done, 8)
            dve.tensor_scalar(cols[:, 4:5], cols[:, 1:2], part[:, 1:2], -1.0, ALU.add, ALU.add).then_inc(prep_done, 1)
            dve.scalar_tensor_tensor(out=cols[:, 3:4], in0=cols[:, 1:2], scalar=float(COLS),
                                     in1=cols[:, 2:3], op0=ALU.is_equal, op1=ALU.mult).then_inc(prep_done, 1)
            dve.tensor_tensor(restart[:, 1:COLS], dst_t[:, 1:COLS], dst_t[:, 0:COLS - 1],
                              ALU.not_equal).then_inc(prep_done, 1)
            dve.wait_ge(prep_done, 11)
            dve.tensor_copy(patch_row[:, :], cols[:, 4:5]).then_inc(prep_done, 1)
            dve.tensor_scalar(restart[:, 1:COLS], restart[:, 1:COLS], LOWEST, None, ALU.mult).then_inc(prep_done, 1)
            dve.memset(restart[:, 0:1], LOWEST).then_inc(prep_done, 1)
            dve.tensor_scalar(diag[:, 0, :], ident[:, :], cols[:, 2:3], None, ALU.mult).then_inc(join_diag, 1)
            dve.tensor_scalar(diag[:, 1, :], ident[:, :], cols[:, 3:4], None, ALU.mult).then_inc(join_diag, 1)
            dve.wait_ge(join_spread, 1)
            dve.tensor_scalar(join_row[:, :, :].rearrange("p a b -> p (a b)"), carry_ps[:, 0:2 * P],
                              -LOWEST, LOWEST, ALU.mult, ALU.add).then_inc(join_diag, 1)

            for l, (w, n) in enumerate(shapes):
                kc = w // P
                dve.wait_ge(const_done, CONSTS)
                if l:
                    dve.wait_ge(index_staged, STAGED * l)
                if l:
                    stage_first_step()
                with dve.Fori(0, STEPS) as i:
                    for b in range(BLOCKS):
                        dve.wait_ge(landed[b], i * (DMA * BLOCK_COLS) + DMA * BLOCK_COLS * (STEPS * l + 1))
                        dve.wait_ge(edges_loaded, 3 * DMA)
                        dve.tensor_copy(
                            index_stage[:, b, :],
                            src_t[:, bass.ds(i * RING_COLS + (RING_COLS + b * BLOCK_COLS), BLOCK_COLS)],
                        ).then_inc(index_staged, 1)
                        if l == 0:
                            dve.wait_ge(hot_used[b], i + 1)
                        for u in range(BLOCK_COLS):
                            c = b * BLOCK_COLS + u
                            here = ring[:, c * w:(c + 1) * w]
                            before = ring[:, (c - 1) * w:c * w] if c else carry[:, 0:w]
                            dve.wait_ge(scan_done, i * SCANS_STEP + (SCANS * l + c + 1))
                            dve.scalar_tensor_tensor(
                                out=here, in0=before, scalar=restart[:, bass.ds(i * RING_COLS + c, 1)],
                                in1=here, op0=ALU.add, op1=ALU.max).then_inc(scan_done, 1)
                            if l == 0:
                                dve.tensor_scalar(hot[:, c, 0:P], lane_bf[:, :],
                                                  dst_lane[:, bass.ds(i * RING_COLS + c, 1)], None,
                                                  ALU.is_equal).then_inc(hot_ready, 1)
                                dve.tensor_scalar(hot[:, c, P:HOT], lane_bf[:, 0:TILES],
                                                  dst_tile[:, bass.ds(i * RING_COLS + c, 1)], None,
                                                  ALU.is_equal).then_inc(hot_ready, 1)
                    dve.wait_ge(scan_done, i * SCANS_STEP + (SCANS * l + RING_COLS + 1))
                    dve.tensor_copy(carry[:, 0:w], ring[:, (RING_COLS - 1) * w:RING_COLS * w]
                                    ).then_inc(scan_done, 1)

                if l == 0:
                    dve.wait_ge(count_ready, 1)
                    dve.tensor_copy(count[:, :], hist_ps[:, 0:TILES]).then_inc(ends_step, 1)
                    dve.wait_ge(count_spread, 1)
                    dve.tensor_copy(total[:, :], hist_ps[:, TILES:2 * TILES]).then_inc(ends_step, 1)
                    dve.wait_ge(ends_step, 2)
                    dve.tensor_tensor_scan(upto[:, :], total[:, :], zero_tiles[:, :], 0.0,
                                           ALU.add, ALU.add).then_inc(ends_step, 1)
                    dve.wait_ge(ends_step, 3)
                    dve.tensor_tensor(total[:, :], upto[:, :], total[:, :], ALU.subtract).then_inc(ends_step, 1)
                    dve.wait_ge(ends_step, 4)
                    dve.scalar_tensor_tensor(out=ends[:, :], in0=hist_ps[:, 0:TILES],
                                             scalar=-float(1 + P * COLS), in1=total[:, :],
                                             op0=ALU.add, op1=ALU.add).then_inc(ends_step, 1)
                    dve.wait_ge(ends_step, 5)
                    dve.scalar_tensor_tensor(out=upto[:, :], in0=count[:, :], scalar=0.0,
                                             in1=ends[:, :], op0=ALU.is_gt, op1=ALU.mult).then_inc(ends_step, 1)
                    dve.wait_ge(ends_step, 6)
                    dve.tensor_scalar(end_row[:, 0:TILES], upto[:, :], float(P * COLS), None,
                                      ALU.add).then_inc(ends_step, 1)

                dve.wait_ge(carry_turned, l + 1)
                dve.wait_ge(join_diag, 3)
                for c in range(kc):
                    dve.tensor_tensor_scan(carry_scan[:, c, :], join_row[:, 1, :],
                                           carry_ps[:, c * P:(c + 1) * P], 0.0,
                                           ALU.add, ALU.max).then_inc(join_step, 1)
                for c in range(kc):
                    before = sum(s[0] for s in shapes[:l]) // P
                    dve.wait_ge(join_step, before + c + 1)
                    dve.tensor_tensor(incoming[:, c, 1:P], carry_scan[:, c, 0:P - 1],
                                      join_row[:, 0, 1:P], ALU.add).then_inc(incoming_ready, 1)
                dve.wait_ge(incoming_turned, l + 1)
                dve.wait_ge(patch_landed, DMA * (l + 1))
                dve.tensor_tensor(patch[:, 0:w], patch[:, 0:w], back_ps[:, 0:w], ALU.max).then_inc(patched, 1)

                def stage_ends(h, tile):
                    at = tile + SHARES[h]
                    size = SHARES[h + 1] - SHARES[h]
                    dve.tensor_copy(end_stage[h][:, :], end_row[:, bass.ds(at, size)]).then_inc(end_staged, 1)

                def mask(i, q):
                    b = BUFFERS[q % TAIL_PAIRS]
                    dve.wait_ge(agg_turned, i * TAIL_PAIRS + (PAIRS * l + q + 1))
                    dve.tensor_scalar(finite[b][:, 0:2 * w], turn_ps[b][:, 0:2 * w].bitcast(I32),
                                      TOP_EXPONENT, TOP_EXPONENT, ALU.bitwise_and, ALU.bitwise_xor
                                      ).then_inc(mask_done, 1)

                def guard(i, q):
                    b = BUFFERS[q % TAIL_PAIRS]
                    dve.wait_ge(mask_done, i * TAIL_PAIRS + (PAIRS * l + q + 1))
                    dve.wait_ge(agg_zeroed, i * TAIL_PAIRS + (PAIRS * l + q + 4 - REUSE[q % TAIL_PAIRS]))
                    dve.sem_inc(guard_open, 1)
                    dve.copy_predicated(agg[b][:, 0:2 * w], finite[b][:, 0:2 * w], turn_ps[b][:, 0:2 * w]
                                        ).then_inc(agg_done, 1)

                def add_own(i, q):
                    dve.wait_ge(z_ready, i * TAIL_PAIRS + (PAIRS * l + q + 1))
                    dve.tensor_tensor(z_sum[BUFFERS[q]][:, 0:2 * n], mm_ps[BUFFERS[q]][:, 0:2 * n],
                                      own[:, bass.ds(i * (TAIL_TILES * n) + q * (2 * n), 2 * n)],
                                      ALU.add).then_inc(sum_done, 1)

                def finish(i, q, first):
                    if not first:
                        dve.wait_ge(h_stored[q], i * DMA + PER_OUT * l)
                    dve.wait_ge(sum_done, i * TAIL_PAIRS + (PAIRS * l + q + 1))
                    made = dve.scalar_tensor_tensor(out=h_out[q][:, 0:2 * n], in0=z_sum[BUFFERS[q]][:, 0:2 * n],
                                                    scalar=SLOPE, in1=z_sum[BUFFERS[q]][:, 0:2 * n],
                                                    op0=ALU.mult, op1=ALU.max)
                    if l < LAYERS - 1:
                        made.then_inc(h_done, 1)
                    else:
                        made.then_inc(act_done, 1)
                        dve.wait_ge(act_done, i * TAIL_PAIRS + (q + 1))
                        dve.tensor_tensor(h_out[q][:, 0:2 * n], h_out[q][:, 0:2 * n],
                                          own[:, bass.ds(i * (TAIL_TILES * n) + (TILES * n + q * 2 * n), 2 * n)],
                                          ALU.add).then_inc(h_done, 1)

                dve.wait_ge(ends_step, ENDS)
                if l:
                    dve.wait_ge(end_staged, 2 * (TAIL_STEPS + 1) * l)
                stage_ends(0, 0)
                stage_ends(1, 0)
                dve.wait_ge(own_done, TILES * (l + 1))
                if l == LAYERS - 1:
                    dve.wait_ge(residual_loaded, DMA)

                def tail(i, first, last):
                    for q in range(1, TAIL_PAIRS + 1 - last):
                        mask(i, q)
                        if 2 * q + 2 in SHARES:
                            stage_ends(SHARES.index(2 * q + 2) - 1, i * TAIL_TILES + TAIL_TILES)
                        guard(i, q)
                        add_own(i, q - 1)
                        finish(i, q - 1, first)
                    if last:
                        add_own(i, TAIL_PAIRS - 1)
                        finish(i, TAIL_PAIRS - 1, first)

                mask(0, 0)
                guard(0, 0)
                if l == 0:
                    tail(0, True, False)
                with dve.Fori(1 if l == 0 else 0, TAIL_STEPS - 1) as i:
                    tail(i, False, False)
                tail(TAIL_STEPS - 1, False, True)

        @block.tensor
        def _(pe):
            for b in range(BLOCKS):
                pe.sem_inc(hot_used[b], 1)
            pe.wait_ge(order_checked, 3)
            pe.matmul(back_ps[:, 0:1], ones[:, :], cols[:, 5:6], start=True, stop=True).then_inc(order_summed, 1)
            pe.wait_ge(join_diag, 2)
            for f in range(2):
                mm = pe.matmul(carry_ps[:, f * P:(f + 1) * P], ones[:, :], diag[:, f, :],
                               start=True, stop=True)
            mm.then_inc(join_spread, 1)
            pe.wait_ge(weights_loaded, N_WEIGHTS)

            for l, (w, n) in enumerate(shapes):
                kc = w // P

                def own_pair(j):
                    for p in range(2):
                        pe.wait_ge(in_loaded[p], j * DMA + DMA * (PAIRS * l + 1))
                        for c in range(kc):
                            turn = pe.transpose(turn_ps[p][:, c * P:(c + 1) * P],
                                                h_in[p][:, c * P:(c + 1) * P], ident[:, :])
                        turn.then_inc(in_turned, 1)
                        pe.wait_ge(in_copied, j * 2 + (TILES * l + p + 1))
                        for c in range(kc):
                            pe.matmul(mm_ps[p][:, 0:n], h_turned[p][:, c, :], wr_sb[l][:, c, :],
                                      start=(c == 0), stop=False)
                        pe.matmul(mm_ps[p][:, 0:n], ones[0:1, :], b_sb[l][:, :],
                                  start=False, stop=True).then_inc(own_mm, 1)

                def histogram(i):
                    for b in range(BLOCKS):
                        pe.wait_ge(hot_ready, i * (2 * RING_COLS) + 2 * (b + 1) * BLOCK_COLS)
                        for u in range(BLOCK_COLS):
                            c = b * BLOCK_COLS + u
                            mm = pe.matmul(hist_ps[:, 0:TILES], hot[:, c, 0:P], hot[:, c, P:HOT],
                                           start=False, stop=False, skip_group_check=True)
                        mm.then_inc(hot_used[b], 1)

                if l == 0:
                    pe.wait_ge(const_done, CONSTS)
                    pe.matmul(hist_ps[:, 0:TILES], no_hot[:, 0:P], no_hot[:, P:HOT],
                              start=True, stop=False, skip_group_check=True)
                    with pe.Fori(0, PAIRS) as i:
                        histogram(i)
                        own_pair(i)
                    if STEPS > PAIRS:
                        with pe.Fori(PAIRS, STEPS) as i:
                            histogram(i)
                    pe.matmul(hist_ps[:, 0:TILES], no_hot[:, 0:P], no_hot[:, P:HOT],
                              start=False, stop=True, skip_group_check=True).then_inc(count_ready, 1)
                    pe.wait_ge(ends_step, 1)
                    pe.matmul(hist_ps[:, 0:TILES], upper[:, :], count[:, :], start=True, stop=True)
                    pe.matmul(hist_ps[:, TILES:2 * TILES], ones[:, :], count[:, :],
                              start=True, stop=True).then_inc(count_spread, 1)
                else:
                    with pe.Fori(0, PAIRS) as i:
                        own_pair(i)

                pe.wait_ge(scan_done, SCANS * (l + 1) + 1)
                for c in range(kc):
                    turn = pe.transpose(carry_ps[:, c * P:(c + 1) * P], carry[:, c * P:(c + 1) * P],
                                        ident[:, :])
                turn.then_inc(carry_turned, 1)
                pe.wait_ge(incoming_ready, sum(s[0] for s in shapes[:l + 1]) // P)
                for c in range(kc):
                    turn = pe.transpose(back_ps[:, c * P:(c + 1) * P], incoming[:, c, :], ident[:, :])
                turn.then_inc(incoming_turned, 1)

                def turn_pair(i, q):
                    b = BUFFERS[q % TAIL_PAIRS]
                    for t in range(2):
                        k = (2 * q + t) % TAIL_TILES
                        pe.wait_ge(end_landed[k], i * DMA + DMA * (TAIL_STEPS * l + q // TAIL_PAIRS + 1))
                        for c in range(kc):
                            turn = pe.transpose(turn_ps[b][:, t * w + c * P:t * w + (c + 1) * P],
                                                ring[:, k * w + c * P:k * w + (c + 1) * P], ident[:, :])
                    turn.then_inc(agg_turned, 1)

                def project_pair(i, q):
                    b = BUFFERS[q]
                    pe.wait_ge(agg_done, i * TAIL_PAIRS + (PAIRS * l + q + 1))
                    for t in range(2):
                        for c in range(kc):
                            mm = pe.matmul(mm_ps[b][:, t * n:(t + 1) * n],
                                           agg[b][:, t * w + c * P:t * w + (c + 1) * P],
                                           wl_sb[l][:, c, :], start=(c == 0), stop=(c == kc - 1))
                    mm.then_inc(z_ready, 1)

                def tail(i, last):
                    for q in range(1, TAIL_PAIRS + 1 - last):
                        turn_pair(i, q)
                        project_pair(i, q - 1)
                    if last:
                        project_pair(i, TAIL_PAIRS - 1)

                pe.wait_ge(own_done, TILES * (l + 1))
                turn_pair(0, 0)
                with pe.Fori(0, TAIL_STEPS - 1) as i:
                    tail(i, False)
                tail(TAIL_STEPS - 1, True)

        @block.scalar
        def _(act):
            def deviation(s):
                t = slice(s * TAIL_TILES, (s + 1) * TAIL_TILES)
                act.wait_ge(var_done, TAIL_TILES * (s + 1))
                nc.scalar.activation(std[:, t], mean_var[:, t, 1], ACT.Sqrt, bias=eps[:, 0:1]).then_inc(std_done, 1)

            act.wait_ge(const_done, CONSTS)
            deviation(0)
            for s in range(TAIL_STEPS):
                if s < TAIL_STEPS - 1:
                    deviation(s + 1)
                act.wait_ge(norm_ready, 2 * (s + 1))
                for k in range(s * TAIL_TILES, s * TAIL_TILES + ACT_TILES):
                    nc.scalar.activation(h0_all[:, k, :], x_all[:, k, :], ACT.Relu, bias=shift[:, k:k + 1],
                                         scale=rstd[:, k:k + 1]).then_inc(h0_done, 1)

            for b in range(3):
                nc.scalar.activation(agg[b][:, :], zeros[:, :], ACT.Copy).then_inc(agg_zeroed, 1)

            for l, (w, n) in enumerate(shapes):
                if l == 0:
                    act.wait_ge(h0_stored, DMA * TAIL_STEPS)
                else:
                    for b in range(TAIL_PAIRS):
                        act.wait_ge(h_stored[b], PER_OUT * l)
                if l == LAYERS - 1:
                    act.dma_start(own[:, TILES * n:TILES * (n + F_IN)].rearrange("p (t f) -> p t f", f=F_IN),
                                  x.rearrange("(t p) f -> p t f", p=P)).then_inc(residual_loaded, DMA)

                def load(tile, p):
                    act.dma_start(h_in[p][:, 0:w], tables[l][bass.ds(tile * P, P), :]).then_inc(in_loaded[p], DMA)

                def copy_pair(j, more):
                    for p in range(2):
                        act.wait_ge(in_turned, j * 2 + (TILES * l + p + 1))
                        nc.scalar.activation(h_turned[p][:, :, :].rearrange("p c m -> p (c m)")[:, 0:w],
                                             turn_ps[p][:, 0:w], ACT.Copy).then_inc(in_copied, 1)
                        if more:
                            load(j * 2 + (p + 2), p)
                        act.wait_ge(own_mm, j * 2 + (TILES * l + p + 1))
                        act.wait_ge(weights_loaded, N_WEIGHTS)
                        nc.scalar.activation(own[:, bass.ds(j * (2 * n) + p * n, n)], mm_ps[p][:, 0:n],
                                             ACT.Copy).then_inc(own_done, 1)

                load(0, 0)
                load(1, 1)
                with act.Fori(0, PAIRS - 1) as j:
                    copy_pair(j, True)
                copy_pair(PAIRS - 1, False)
                with act.Fori(0, TAIL_STEPS) as i:
                    for q in range(TAIL_PAIRS):
                        act.wait_ge(z_ready, i * TAIL_PAIRS + (PAIRS * l + q + 1))
                        nc.scalar.activation(agg[BUFFERS[q]][:, :], zeros[:, :], ACT.Copy).then_inc(agg_zeroed, 1)

        @block.sync
        def _(sp):
            x_rows = x.rearrange("(t p) f -> p t f", p=P)
            h0_rows = tables[0].rearrange("(t p) f -> p t f", p=P)
            for s in range(TAIL_STEPS):
                t = slice(s * TAIL_TILES, (s + 1) * TAIL_TILES)
                sp.dma_start(x_all[:, t, :], x_rows[:, t, :]).then_inc(x_loaded[s], DMA)
                if s == 0:
                    sp.dma_start(dst_t[:, :], dst).then_inc(edges_loaded, DMA)
                    with nc.allow_non_contiguous_dma(reason="one word of each partition's run of edges"):
                        sp.dma_start(prev_last[1:P, :], dst[0:P - 1, COLS - 1:COLS]).then_inc(edges_loaded, DMA)
            sp.dma_start(src_t[:, 0:COLS], src).then_inc(edges_loaded, DMA)
            for l, (wl, bl, wr) in enumerate(weights):
                sp.dma_start(wr_sb[l][:, :, :], wr.rearrange("(c p) n -> p c n", p=P)).then_inc(weights_loaded, DMA)
                sp.dma_start(wl_sb[l][:, :, :], wl.rearrange("(c p) n -> p c n", p=P)).then_inc(weights_loaded, DMA)
                sp.dma_start(b_sb[l][:, :], bl.rearrange("(a n) -> a n", a=1)).then_inc(weights_loaded, DMA)
            sp.wait_ge(const_done, CONSTS)
            for w in widths:
                sp.dma_start(logs[w][P * COLS:LOG_ROWS, :], empty_row[:, 0:w]).then_inc(empty_stored, DMA)
            for s in range(TAIL_STEPS):
                t = slice(s * TAIL_TILES, (s + 1) * TAIL_TILES)
                sp.wait_ge(h0_done, ACT_TILES * (s + 1))
                sp.wait_ge(h0_rest_done, s + 1)
                sp.dma_start(h0_rows[:, t, :], h0_all[:, t, :]).then_inc(h0_stored, DMA)

            for l, (w, n) in enumerate(shapes):
                with sp.Fori(0, STEPS) as i:
                    for b in range(BLOCKS):
                        sp.wait_ge(scan_done, i * SCANS_STEP + (SCANS * l + (b + 1) * BLOCK_COLS + 2))
                        c = b * BLOCK_COLS
                        sp.dma_start(log_block(l, i, b), ring[:, c * w:(c + BLOCK_COLS) * w]).then_inc(logged[b], DMA)
                made = tables[l + 1] if l < LAYERS - 1 else out
                with sp.Fori(0, TAIL_STEPS) as i:
                    for q in range(TAIL_PAIRS):
                        sp.wait_ge(h_done, i * TAIL_PAIRS + (PAIRS * l + q + 1))
                        rows = made[bass.ds(i * (TAIL_TILES * P) + q * (2 * P), 2 * P), :]
                        sp.dma_start(rows.rearrange("(t p) f -> p t f", p=P),
                                     h_out[q][:, 0:2 * n].rearrange("p (t f) -> p t f", f=n)
                                     ).then_inc(h_stored[q], DMA)
            for b in range(TAIL_PAIRS):
                sp.wait_ge(h_stored[b], PER_OUT * LAYERS)


def kernel(**inputs):
    import numpy as np
    import concourse.bacc as bacc
    from concourse.bass_utils import run_bass_kernel_spmd

    x = np.ascontiguousarray(inputs["x"])
    nodes, features = x.shape
    edges = inputs["src"].shape[0]
    group = P * TAIL_TILES
    rows = -(-nodes // group) * group
    cols = -(-edges // (P * RING_COLS)) * RING_COLS

    def filled(a, size, fill):
        whole = np.full(size, fill, a.dtype)
        whole[:a.shape[0]] = a
        return whole.reshape(P, -1)

    x_rows = np.zeros((rows, features), x.dtype)
    x_rows[:nodes] = x
    arrays = {
        "x": x_rows,
        "src": filled(np.asarray(inputs["src"]), P * cols, 0),
        "dst": filled(np.asarray(inputs["dst"]), P * cols, NO_NODE),
    }
    layers = [f"L0_gnn_{part}{l}" for l in (1, 2, 3) for part in ("Wl", "bl", "Wr")]
    for name in layers:
        arrays[name] = np.ascontiguousarray(inputs[name])
    nc = bacc.Bacc("TRN2", target_bir_lowering=False, num_devices=1)
    given = {
        name: nc.dram_tensor(name, a.shape, mybir.dt.from_np(a.dtype), kind="ExternalInput").ap()
        for name, a in arrays.items()
    }
    out = nc.dram_tensor("out", (rows, arrays["L0_gnn_Wl3"].shape[1]), F32, kind="ExternalOutput").ap()
    weights = [tuple(given[name] for name in layers[3 * l:3 * l + 3]) for l in range(3)]
    gnn_program(nc, given["x"], given["src"], given["dst"], weights, out)
    r = run_bass_kernel_spmd(nc, [arrays], core_ids=[0])
    return r.results[0]["out"][:nodes]
```

```python
from contextlib import ExitStack

import concourse.bass as bass
from concourse import mybir

ALU = mybir.AluOpType
ACT = mybir.ActivationFunctionType
AXIS = mybir.AxisListType
F32 = mybir.dt.float32
BF16 = mybir.dt.bfloat16
I32 = mybir.dt.int32
U32 = mybir.dt.uint32

P = 128
LANE_BITS = 7
BLOCKS = 9
BLOCK_COLS = 6
RING_COLS = BLOCKS * BLOCK_COLS
TAIL_TILES = 10
TAIL_PAIRS = TAIL_TILES // 2
SHARES = (0, 4, TAIL_TILES)
BUFFERS = (0, 1, 0, 1, 2)
REUSE = tuple(next(d for d in range(1, TAIL_PAIRS + 1) if BUFFERS[q - d] == BUFFERS[q])
              for q in range(TAIL_PAIRS))
ACT_TILES = 8
DMA = 16
LOWEST = -3.4028234663852886e38
TOP_EXPONENT = 0x7F000000
SLOPE = 0.01
EPS = 1e-5
NO_NODE = 1 << 20


def gnn_program(nc, x, src, dst, weights, out):
    NODES, F_IN = x.shape
    COLS = src.shape[1]
    TILES = NODES // P
    STEPS = -(-COLS // RING_COLS)
    LAST = COLS - (STEPS - 1) * RING_COLS
    TAIL_STEPS = TILES // TAIL_TILES
    PAIRS = TILES // 2
    assert TILES % TAIL_TILES == 0
    assert PAIRS < STEPS
    shapes = [wl.shape for wl, _, _ in weights]
    F_MAX = max(max(s) for s in shapes)
    KC_MAX = F_MAX // P
    LOG_ROWS = P * COLS + 1
    SCANS_STEP = RING_COLS + 1
    SCANS = (STEPS - 1) * SCANS_STEP + LAST + 1
    STAGED = STEPS * BLOCKS

    def width(b, last):
        return max(0, min(BLOCK_COLS, LAST - b * BLOCK_COLS)) if last else BLOCK_COLS

    def used_blocks(last):
        return [b for b in range(BLOCKS) if width(b, last)]

    LANDED = [DMA * ((STEPS - 1) * BLOCK_COLS + width(b, True)) for b in range(BLOCKS)]
    LOGGED = [DMA * (STEPS - 1 + (width(b, True) > 0)) for b in range(BLOCKS)]

    tables = [nc.dram_tensor(f"features_{l}", (NODES, s[0]), F32).ap() for l, s in enumerate(shapes)]
    widths = sorted({s[0] for s in shapes})
    logs = {w: nc.dram_tensor(f"running_max_log_{w}", (LOG_ROWS, w), F32).ap() for w in widths}

    with ExitStack() as ctx:
        def sb(name, shape, dt=F32):
            return ctx.enter_context(nc.sbuf_tensor(name, shape, dt))

        def ps(name, shape, dt=F32):
            return ctx.enter_context(nc.psum_tensor(name, shape, dt))

        def sem(name):
            return ctx.enter_context(nc.semaphore(name))

        ring = sb("ring", [P, RING_COLS * F_MAX])
        second = RING_COLS * F_IN
        x_all = ring[:, 0:TILES * F_IN].rearrange("p (t f) -> p t f", f=F_IN)
        h0_all = ring[:, second:second + TILES * F_IN].rearrange("p (t f) -> p t f", f=F_IN)
        HOT = P + TILES
        HOT_WORDS = RING_COLS * HOT // 2
        assert second >= TILES * F_IN and second + max(TILES * F_IN, HOT_WORDS) <= RING_COLS * F_MAX
        hot = ring[:, second:second + HOT_WORDS].bitcast(BF16).rearrange("p (c h) -> p c h", h=HOT)

        own = sb("own", [P, TILES * F_MAX])
        src_t = sb("src_t", [P, STEPS * RING_COLS], I32)
        dst_t = sb("dst_t", [P, COLS], I32)
        restart = sb("restart", [P, COLS])
        dst_lane = sb("dst_lane", [P, COLS], BF16)
        dst_tile = sb("dst_tile", [P, COLS], BF16)
        index_stage = sb("index_stage", [P, BLOCKS, BLOCK_COLS], I32)
        end_row = sb("end_row", [P, TILES + TAIL_TILES], I32)
        end_stage = [sb(f"end_stage{h}", [P, SHARES[h + 1] - SHARES[h]], I32) for h in range(2)]
        wl_sb, wr_sb, b_sb = [], [], []
        for l, (k, n) in enumerate(shapes):
            wl_sb.append(sb(f"wl{l}", [P, k // P, n]))
            wr_sb.append(sb(f"wr{l}", [P, k // P, n]))
            b_sb.append(sb(f"b{l}", [1, n]))
        lane_i = sb("lane_i", [P, P], I32)
        lane = sb("lane", [P, P])
        lane_bf = sb("lane_bf", [P, P], BF16)
        part_i = sb("part_i", [P, 2], I32)
        part = sb("part", [P, 2])
        ident = sb("ident", [P, P])
        upper = sb("upper", [P, P])
        ones = sb("ones", [P, P])
        prev_last = sb("prev_last", [P, 1], I32)
        cols = sb("cols", [P, 8])
        patch_row = sb("patch_row", [P, 1], I32)
        diag = sb("diag", [P, 2, P])
        join_row = sb("join_row", [P, 2, P])
        stats = sb("stats", [P, TAIL_TILES, 6])
        mean_var = sb("mean_var", [P, TILES, 2])
        std = sb("std", [P, TILES])
        rstd = sb("rstd", [P, TILES])
        shift = sb("shift", [P, TILES])
        eps = sb("eps", [P, 1])
        unsorted = sb("unsorted", [P, 1], I32)
        count = sb("count", [P, TILES])
        total = sb("total", [P, TILES])
        zeros = sb("zeros", [P, 2 * F_MAX])
        empty_row = sb("empty_row", [1, F_MAX])
        no_hot = sb("no_hot", [P, HOT], BF16)
        upto = sb("upto", [P, TILES])
        ends = sb("ends", [P, TILES])
        zero_tiles = sb("zero_tiles", [P, TILES])
        h_in = [sb(f"h_in{b}", [P, F_MAX]) for b in range(2)]
        h_turned = [sb(f"h_turned{b}", [P, KC_MAX, P]) for b in range(2)]
        agg = [sb(f"agg{b}", [P, 2 * F_MAX]) for b in range(3)]
        finite = [sb(f"finite{b}", [P, 2 * F_MAX], I32) for b in range(3)]
        z_sum = [sb(f"z_sum{b}", [P, 2 * F_MAX]) for b in range(3)]
        h_out = [sb(f"h_out{k}", [P, 2 * F_MAX]) for k in range(TAIL_PAIRS)]
        carry = sb("carry", [P, F_MAX])
        carry_scan = sb("carry_scan", [P, KC_MAX, P])
        incoming = sb("incoming", [P, KC_MAX, P])
        patch = sb("patch", [P, F_MAX])

        turn_ps = [ps(f"turn_ps{b}", [P, 512]) for b in range(3)]
        mm_ps = [ps(f"mm_ps{b}", [P, 512]) for b in range(3)]
        hist_ps = mm_ps[2]
        carry_ps = ps("carry_ps", [P, 512])
        back_ps = ps("back_ps", [P, 512])

        x_loaded = [sem(f"x_loaded{s}") for s in range(TAIL_STEPS)]
        edges_loaded, weights_loaded = sem("edges_loaded"), sem("weights_loaded")
        iota_done, const_done, prep_done = sem("iota_done"), sem("const_done"), sem("prep_done")
        stats_done, var_done, std_done, norm_ready = (
            sem("stats_done"), sem("var_done"), sem("std_done"), sem("norm_ready"))
        h0_scaled, h0_rest_done = sem("h0_scaled"), sem("h0_rest_done")
        h0_done, h0_stored, empty_stored = sem("h0_done"), sem("h0_stored"), sem("empty_stored")
        join_diag, join_spread = sem("join_diag"), sem("join_spread")
        index_staged, gathers_open = sem("index_staged"), sem("gathers_open")
        landed = [sem(f"landed{b}") for b in range(BLOCKS)]
        scan_done = sem("scan_done")
        logged = [sem(f"logged{b}") for b in range(BLOCKS)]
        hot_ready, hot_used = sem("hot_ready"), [sem(f"hot_used{b}") for b in range(BLOCKS)]
        count_ready, count_spread, ends_step = sem("count_ready"), sem("count_spread"), sem("ends_step")
        in_loaded = [sem(f"in_loaded{b}") for b in range(2)]
        in_turned, in_copied, own_mm, own_done = (
            sem("in_turned"), sem("in_copied"), sem("own_mm"), sem("own_done"))
        carry_turned, join_step, incoming_ready, incoming_turned = (
            sem("carry_turned"), sem("join_step"), sem("incoming_ready"), sem("incoming_turned"))
        patch_landed, patched, patch_stored = sem("patch_landed"), sem("patched"), sem("patch_stored")
        end_staged = sem("end_staged")
        end_landed = [sem(f"end_landed{k}") for k in range(TAIL_TILES)]
        agg_turned, mask_done, guard_open, agg_done = (
            sem("agg_turned"), sem("mask_done"), sem("guard_open"), sem("agg_done"))
        z_ready, sum_done, act_done, h_done = (
            sem("z_ready"), sem("sum_done"), sem("act_done"), sem("h_done"))
        agg_zeroed = sem("agg_zeroed")
        h_stored = [sem(f"h_stored{k}") for k in range(TAIL_PAIRS)]
        residual_loaded = sem("residual_loaded")

        BINS = NODES + 1
        SLOTS = BINS + P
        next_row = nc.dram_tensor("sort_next_row", (SLOTS, 1), F32).ap()
        sorted_src = nc.dram_tensor("sorted_src", (P * COLS, 1), I32).ap()
        sorted_dst = nc.dram_tensor("sorted_dst", (P * COLS, 1), I32).ap()
        assert 2 * SLOTS <= RING_COLS * F_MAX
        bin_counts, bin_starts = ring[0:1, 0:SLOTS], ring[0:1, SLOTS:2 * SLOTS]
        s_dst_row = ring[:, 0:P].bitcast(I32)
        s_key_row, s_equal, s_prior = ring[:, P:2 * P], ring[:, 2 * P:3 * P], ring[:, 3 * P:4 * P]
        s_int = ring[:, 4 * P:4 * P + 8].bitcast(I32)
        s_f = ring[:, 4 * P + 8:4 * P + 16]
        order_checked, order_summed, unsorted_known = (
            sem("order_checked"), sem("order_summed"), sem("unsorted_known"))
        sort_loaded = [sem(f"sort_loaded_{what}") for what in ("dst_row", "dst", "src")]
        sort_put = [sem(f"sort_put_{what}") for what in ("next_row", "src", "dst")]
        sort_free, sort_keyed, sort_fetched = sem("sort_free"), sem("sort_keyed"), sem("sort_fetched")
        sort_placed, sort_v, sort_open = sem("sort_placed"), sem("sort_v"), sem("sort_open")
        assert 2 * COLS * DMA < 1 << 16
        sort_bins, sort_done = sem("sort_bins"), sem("sort_done")
        sort_w, sort_x = sem("sort_w"), sem("sort_x")

        LAYERS = len(shapes)
        CONSTS = 15
        PREP = 14
        ENDS = 7
        N_WEIGHTS = 3 * LAYERS * DMA
        PER_OUT = TAIL_STEPS * DMA

        def log_block(l, step, b, columns):
            w = shapes[l][0]
            body = logs[w][0:P * COLS, :].rearrange("(p c) f -> p (c f)", p=P)
            return body[:, bass.ds((step * BLOCKS + b) * (BLOCK_COLS * w), columns * w)]

        block = ctx.enter_context(nc.Block())

        @block.gpsimd
        def _(pool):
            pool.iota(lane_i[:, :], [[1, P]], base=0, channel_multiplier=0).then_inc(iota_done, 1)
            pool.iota(part_i[:, 0:1], [[0, 1]], base=0, channel_multiplier=1).then_inc(iota_done, 1)
            pool.iota(part_i[:, 1:2], [[0, 1]], base=0, channel_multiplier=COLS).then_inc(iota_done, 1)

            def sort_group(g, place):
                n = g + COLS if place else g
                pool.wait_ge(sort_free, n + 1)
                flat = dst.rearrange("p c -> (p c)")
                pool.dma_start(s_dst_row, flat[bass.ds(g * P, P)].partition_broadcast(P)
                               ).then_inc(sort_loaded[0], DMA)
                with nc.allow_non_contiguous_dma(reason="one edge in each partition"):
                    pool.dma_start(s_int[:, 0:1], flat[bass.ds(g * P, P)].rearrange("(p a) -> p a", a=1)
                                   ).then_inc(sort_loaded[1], DMA)
                    pool.dma_start(s_int[:, 1:2], src.rearrange("p c -> (p c)")[bass.ds(g * P, P)]
                                   .rearrange("(p a) -> p a", a=1)).then_inc(sort_loaded[2], DMA)
                pool.wait_ge(sort_keyed, n + 1)
                pool.sem_inc(sort_open, 1)
                pool.indirect_dma_start(s_f[:, 1:2], None, next_row,
                                        bass.IndirectOffsetOnAxis(ap=s_int[:, 2:3].bitcast(U32), axis=0)
                                        ).then_inc(sort_fetched, DMA)
                pool.wait_ge(sort_placed, n + 1)
                pool.sem_inc(sort_open, 1)
                pool.indirect_dma_start(next_row,
                                        bass.IndirectOffsetOnAxis(ap=s_int[:, 3:4].bitcast(U32), axis=0),
                                        s_f[:, 4:5], None).then_inc(sort_put[0], DMA)
                if place:
                    for k, what, to in ((1, s_int[:, 1:2], sorted_src), (2, s_int[:, 0:1], sorted_dst)):
                        pool.indirect_dma_start(to, bass.IndirectOffsetOnAxis(
                            ap=s_int[:, 4:5].bitcast(U32), axis=0), what, None).then_inc(sort_put[k], DMA)
                pool.wait_ge(sort_put[0], n * DMA + DMA)
                pool.sem_inc(sort_open, 1)

            pool.wait_ge(unsorted_known, 1)
            with pool.If(pool.value_load(unsorted[0:1, 0:1], min_val=0, max_val=1 << 24)):
                next_flat = next_row.rearrange("s a -> a s")
                pool.wait_ge(sort_bins, 1)
                pool.dma_start(next_flat, bin_counts).then_inc(sort_done, DMA)
                pool.wait_ge(sort_done, DMA)
                with pool.Fori(0, COLS) as g:
                    sort_group(g, False)
                pool.wait_ge(sort_free, COLS + 1)
                pool.dma_start(bin_counts, next_flat).then_inc(sort_done, DMA)
                pool.wait_ge(sort_bins, 3)
                pool.dma_start(next_flat, bin_starts).then_inc(sort_done, DMA)
                pool.wait_ge(sort_done, 3 * DMA)
                with pool.Fori(0, COLS) as g:
                    sort_group(g, True)
                pool.wait_ge(sort_put[1], DMA * COLS)
                pool.wait_ge(sort_put[2], DMA * COLS)
                in_runs = sorted_dst.rearrange("(p c) a -> p (c a)", p=P)
                pool.dma_start(dst_t[:, :], in_runs).then_inc(sort_done, DMA)
                pool.dma_start(src_t[:, 0:COLS], sorted_src.rearrange("(p c) a -> p (c a)", p=P)
                               ).then_inc(sort_done, DMA)
                with nc.allow_non_contiguous_dma(reason="one word of each partition's run of edges"):
                    pool.dma_start(prev_last[1:P, :], in_runs[0:P - 1, COLS - 1:COLS]).then_inc(sort_done, DMA)
                pool.wait_ge(sort_done, 6 * DMA)

            for l, (w, _n) in enumerate(shapes):
                if l == 0:
                    pool.wait_ge(h0_stored, DMA * TAIL_STEPS)
                else:
                    for b in range(TAIL_PAIRS):
                        pool.wait_ge(h_stored[b], PER_OUT * l + DMA)

                def gather(i, first, last):
                    for b in used_blocks(last):
                        pool.wait_ge(index_staged, i * BLOCKS + (STAGED * l + b + 1))
                        if not first:
                            pool.wait_ge(logged[b], i * DMA + LOGGED[b] * l)
                        pool.sem_inc(gathers_open, 1)
                        for u in range(width(b, last)):
                            c = b * BLOCK_COLS + u
                            pool.indirect_dma_start(
                                ring[:, c * w:(c + 1) * w], None, tables[l],
                                bass.IndirectOffsetOnAxis(
                                    ap=index_stage[:, b, u:u + 1].bitcast(U32), axis=0),
                            ).then_inc(landed[b], DMA)

                if l == 0:
                    gather(0, True, False)
                with pool.Fori(1 if l == 0 else 0, STEPS - 1) as i:
                    gather(i, False, False)
                gather(STEPS - 1, False, True)
                for b in range(BLOCKS):
                    pool.wait_ge(logged[b], LOGGED[b] * (l + 1))
                pool.wait_ge(prep_done, PREP)
                pool.indirect_dma_start(
                    patch[:, 0:w], None, logs[w],
                    bass.IndirectOffsetOnAxis(ap=patch_row[:, 0:1].bitcast(U32), axis=0),
                ).then_inc(patch_landed, DMA)
                pool.wait_ge(patched, l + 1)
                pool.indirect_dma_start(
                    logs[w], bass.IndirectOffsetOnAxis(ap=patch_row[:, 0:1].bitcast(U32), axis=0),
                    patch[:, 0:w], None,
                ).then_inc(patch_stored, DMA)
                pool.wait_ge(patch_stored, DMA * (l + 1))
                pool.wait_ge(empty_stored, DMA * len(widths))
                with pool.Fori(0, TAIL_STEPS) as i:
                    for k in range(TAIL_TILES):
                        h = int(k >= SHARES[1])
                        if k in SHARES:
                            pool.wait_ge(end_staged, i * 2 + (2 * (TAIL_STEPS + 1) * l + h + 1))
                            pool.sem_inc(gathers_open, 1)
                        pool.indirect_dma_start(
                            ring[:, k * w:(k + 1) * w], None, logs[w],
                            bass.IndirectOffsetOnAxis(
                                ap=end_stage[h][:, k - SHARES[h]:k - SHARES[h] + 1].bitcast(U32), axis=0),
                        ).then_inc(end_landed[k], DMA)

        @block.vector
        def _(dve):
            dve.memset(ones[:, :], 1.0).then_inc(const_done, 1)
            dve.memset(eps[:, :], EPS).then_inc(const_done, 1)
            dve.memset(zero_tiles[:, :], 0.0).then_inc(const_done, 1)
            if COLS < STEPS * RING_COLS:
                dve.memset(src_t[:, COLS:STEPS * RING_COLS], 0).then_inc(const_done, 1)
            else:
                dve.sem_inc(const_done, 1)
            dve.memset(end_row[:, TILES:TILES + TAIL_TILES], 0).then_inc(const_done, 1)
            dve.memset(incoming[:, :, :], LOWEST).then_inc(const_done, 1)
            dve.memset(carry[:, :], 0.0).then_inc(scan_done, 1)
            dve.memset(empty_row[:, :], LOWEST).then_inc(const_done, 1)
            dve.memset(no_hot[:, :], 0.0).then_inc(const_done, 1)
            dve.memset(zeros[:, :], 0.0).then_inc(const_done, 1)
            dve.memset(prev_last[0:1, :], -1).then_inc(const_done, 1)
            dve.wait_ge(iota_done, 3)
            dve.tensor_copy(lane[:, :], lane_i[:, :]).then_inc(const_done, 1)
            dve.tensor_copy(lane_bf[:, :], lane_i[:, :]).then_inc(const_done, 1)
            dve.tensor_copy(part[:, :], part_i[:, :]).then_inc(const_done, 1)
            dve.wait_ge(const_done, 13)
            dve.tensor_scalar(ident[:, :], lane[:, :], part[:, 0:1], None, ALU.is_equal).then_inc(const_done, 1)
            dve.tensor_scalar(upper[:, :], lane[:, :], part[:, 0:1], None, ALU.is_ge).then_inc(const_done, 1)

            def statistics(s):
                dve.wait_ge(x_loaded[s], DMA)
                if s:
                    dve.wait_ge(var_done, TAIL_TILES * s)
                for k in range(TAIL_TILES):
                    dve.bn_stats(stats[:, k, :], x_all[:, s * TAIL_TILES + k, :]).then_inc(stats_done, 1)
                dve.wait_ge(stats_done, TAIL_TILES * (s + 1))
                for k in range(TAIL_TILES):
                    dve.bn_aggr(mean_var[:, s * TAIL_TILES + k, :], stats[:, k, :]).then_inc(var_done, 1)

            def normalise(s):
                t = slice(s * TAIL_TILES, (s + 1) * TAIL_TILES)
                dve.wait_ge(std_done, s + 1)
                dve.reciprocal(rstd[:, t], std[:, t]).then_inc(norm_ready, 1)
                dve.wait_ge(norm_ready, 2 * s + 1)
                dve.scalar_tensor_tensor(out=shift[:, t], in0=mean_var[:, t, 0], scalar=-1.0,
                                         in1=rstd[:, t], op0=ALU.mult, op1=ALU.mult).then_inc(norm_ready, 1)
                own_share = slice(s * TAIL_TILES + ACT_TILES, (s + 1) * TAIL_TILES)
                dve.wait_ge(norm_ready, 2 * s + 2)
                for k in range(own_share.start, own_share.stop):
                    dve.tensor_scalar(h0_all[:, k, :], x_all[:, k, :], rstd[:, k:k + 1], shift[:, k:k + 1],
                                      ALU.mult, ALU.add).then_inc(h0_scaled, 1)
                dve.wait_ge(h0_scaled, (TAIL_TILES - ACT_TILES) * (s + 1))
                dve.tensor_scalar(h0_all[:, own_share, :], h0_all[:, own_share, :], 0.0, None,
                                  ALU.max).then_inc(h0_rest_done, 1)

            for s in range(TAIL_STEPS):
                statistics(s)
                if s:
                    normalise(s - 1)
            normalise(TAIL_STEPS - 1)

            dve.wait_ge(edges_loaded, 3 * DMA)
            dve.tensor_tensor(restart[:, 1:COLS], dst_t[:, 1:COLS], dst_t[:, 0:COLS - 1],
                              ALU.is_lt).then_inc(order_checked, 1)
            dve.tensor_tensor(restart[:, 0:1], dst_t[:, 0:1], prev_last[:, :], ALU.is_lt).then_inc(order_checked, 1)
            dve.wait_ge(order_checked, 2)
            dve.tensor_reduce(cols[:, 5:6], restart[:, :], AXIS.X, ALU.add).then_inc(order_checked, 1)

            def sort_group(g, place):
                n = g + COLS if place else g
                done = 5
                for k in range(3):
                    dve.wait_ge(sort_loaded[k], n * DMA + DMA)
                dve.tensor_scalar(s_key_row, s_dst_row, float(NODES), None, ALU.min).then_inc(sort_v, 1)
                dve.tensor_scalar(s_f[:, 0:1], s_int[:, 0:1], float(NODES), None, ALU.min).then_inc(sort_v, 1)
                dve.wait_ge(sort_v, n * done + 2)
                dve.tensor_copy(s_int[:, 2:3], s_f[:, 0:1]).then_inc(sort_keyed, 1)
                dve.tensor_scalar(s_equal, s_key_row, s_f[:, 0:1], None, ALU.is_equal).then_inc(sort_v, 1)
                dve.wait_ge(sort_v, n * done + 3)
                dve.scalar_tensor_tensor(out=s_prior, in0=lane[:, :], scalar=part[:, 0:1], in1=s_equal,
                                         op0=ALU.is_lt, op1=ALU.mult).then_inc(sort_v, 1)
                dve.tensor_reduce(s_f[:, 3:4], s_equal, AXIS.X, ALU.add).then_inc(sort_v, 1)
                dve.wait_ge(sort_v, n * done + 5)
                dve.tensor_reduce(s_f[:, 2:3], s_prior, AXIS.X, ALU.add).then_inc(sort_w, 1)
                dve.wait_ge(sort_w, n * 4 + 1)
                dve.wait_ge(sort_fetched, n * DMA + DMA)
                dve.tensor_tensor(s_f[:, 4:5], s_f[:, 1:2], s_f[:, 3:4], ALU.add).then_inc(sort_w, 1)
                dve.tensor_tensor(s_int[:, 4:5], s_f[:, 1:2], s_f[:, 2:3], ALU.add).then_inc(sort_w, 1)
                dve.scalar_tensor_tensor(out=s_f[:, 5:6], in0=s_f[:, 2:3], scalar=1.0, in1=s_f[:, 3:4],
                                         op0=ALU.add, op1=ALU.is_equal).then_inc(sort_w, 1)
                dve.wait_ge(sort_w, n * 4 + 4)
                dve.tensor_scalar(s_f[:, 6:7], part[:, 0:1], float(BINS), None, ALU.add).then_inc(sort_x, 1)
                dve.wait_ge(sort_x, n * 3 + 1)
                dve.tensor_tensor(s_f[:, 7:8], s_f[:, 0:1], s_f[:, 6:7], ALU.subtract).then_inc(sort_x, 1)
                dve.wait_ge(sort_x, n * 3 + 2)
                dve.tensor_tensor(s_f[:, 7:8], s_f[:, 7:8], s_f[:, 5:6], ALU.mult).then_inc(sort_x, 1)
                dve.wait_ge(sort_x, n * 3 + 3)
                dve.tensor_tensor(s_int[:, 3:4], s_f[:, 7:8], s_f[:, 6:7], ALU.add).then_inc(sort_placed, 1)
                dve.wait_ge(sort_put[0], n * DMA + DMA)
                if place:
                    dve.wait_ge(sort_put[1], g * DMA + DMA)
                    dve.wait_ge(sort_put[2], g * DMA + DMA)
                dve.sem_inc(sort_free, 1)

            dve.wait_ge(order_summed, 1)
            dve.tensor_copy(unsorted[:, :], back_ps[:, 0:1]).then_inc(unsorted_known, 1)
            dve.wait_ge(unsorted_known, 1)
            with dve.If(dve.value_load(unsorted[0:1, 0:1], min_val=0, max_val=1 << 24)):
                dve.wait_ge(h0_stored, DMA * TAIL_STEPS)
                dve.memset(bin_counts, 0.0).then_inc(sort_bins, 1)
                dve.wait_ge(sort_done, DMA)
                dve.sem_inc(sort_free, 1)
                with dve.Fori(0, COLS) as g:
                    sort_group(g, False)
                dve.wait_ge(sort_done, 2 * DMA)
                dve.memset(bin_starts[:, 0:1], 0.0).then_inc(sort_bins, 1)
                dve.tensor_tensor_scan(bin_starts[:, 1:SLOTS], bin_counts[:, 0:SLOTS - 1],
                                       bin_counts[:, 0:SLOTS - 1], 0.0, ALU.add, ALU.max
                                       ).then_inc(sort_bins, 1)
                dve.wait_ge(sort_done, 3 * DMA)
                with dve.Fori(0, COLS) as g:
                    sort_group(g, True)
                dve.wait_ge(sort_done, 6 * DMA)

            def stage_first_step():
                for b in range(BLOCKS):
                    dve.tensor_copy(index_stage[:, b, :], src_t[:, b * BLOCK_COLS:(b + 1) * BLOCK_COLS]
                                    ).then_inc(index_staged, 1)

            stage_first_step()

            dve.tensor_scalar(restart[:, :].bitcast(I32), dst_t[:, :], P - 1, None,
                              ALU.bitwise_and).then_inc(prep_done, 1)
            dve.wait_ge(prep_done, 1)
            dve.tensor_copy(dst_lane[:, :], restart[:, :].bitcast(I32)).then_inc(prep_done, 1)
            dve.wait_ge(prep_done, 2)
            dve.tensor_scalar(restart[:, :].bitcast(I32), dst_t[:, :], LANE_BITS, None,
                              ALU.arith_shift_right).then_inc(prep_done, 1)
            dve.wait_ge(prep_done, 3)
            dve.tensor_copy(dst_tile[:, :], restart[:, :].bitcast(I32)).then_inc(prep_done, 1)
            dve.tensor_copy(cols[:, 0:1], dst_t[:, 0:1]).then_inc(prep_done, 1)
            dve.wait_ge(prep_done, 5)
            dve.tensor_scalar(restart[:, :], dst_t[:, :], cols[:, 0:1], None, ALU.is_equal).then_inc(prep_done, 1)
            dve.tensor_tensor(cols[:, 2:3], dst_t[:, 0:1], prev_last[:, :], ALU.is_equal).then_inc(prep_done, 1)
            dve.wait_ge(prep_done, 7)
            dve.tensor_reduce(cols[:, 1:2], restart[:, :], AXIS.X, ALU.add).then_inc(prep_done, 1)
            dve.wait_ge(prep_done, 8)
            dve.tensor_scalar(cols[:, 4:5], cols[:, 1:2], part[:, 1:2], -1.0, ALU.add, ALU.add).then_inc(prep_done, 1)
            dve.scalar_tensor_tensor(out=cols[:, 3:4], in0=cols[:, 1:2], scalar=float(COLS),
                                     in1=cols[:, 2:3], op0=ALU.is_equal, op1=ALU.mult).then_inc(prep_done, 1)
            dve.tensor_tensor(restart[:, 1:COLS], dst_t[:, 1:COLS], dst_t[:, 0:COLS - 1],
                              ALU.not_equal).then_inc(prep_done, 1)
            dve.wait_ge(prep_done, 11)
            dve.tensor_copy(patch_row[:, :], cols[:, 4:5]).then_inc(prep_done, 1)
            dve.tensor_scalar(restart[:, 1:COLS], restart[:, 1:COLS], LOWEST, None, ALU.mult).then_inc(prep_done, 1)
            dve.memset(restart[:, 0:1], LOWEST).then_inc(prep_done, 1)
            dve.tensor_scalar(diag[:, 0, :], ident[:, :], cols[:, 2:3], None, ALU.mult).then_inc(join_diag, 1)
            dve.tensor_scalar(diag[:, 1, :], ident[:, :], cols[:, 3:4], None, ALU.mult).then_inc(join_diag, 1)
            dve.wait_ge(join_spread, 1)
            dve.tensor_scalar(join_row[:, :, :].rearrange("p a b -> p (a b)"), carry_ps[:, 0:2 * P],
                              -LOWEST, LOWEST, ALU.mult, ALU.add).then_inc(join_diag, 1)

            for l, (w, n) in enumerate(shapes):
                kc = w // P
                dve.wait_ge(const_done, CONSTS)
                if l:
                    dve.wait_ge(index_staged, STAGED * l)
                    stage_first_step()

                def scan_step(i, last):
                    for b in used_blocks(last):
                        dve.wait_ge(landed[b], i * (DMA * BLOCK_COLS) + (LANDED[b] * l + DMA * width(b, last)))
                        if not last:
                            dve.wait_ge(edges_loaded, 3 * DMA)
                            dve.tensor_copy(
                                index_stage[:, b, :],
                                src_t[:, bass.ds(i * RING_COLS + (RING_COLS + b * BLOCK_COLS), BLOCK_COLS)],
                            ).then_inc(index_staged, 1)
                        if l == 0:
                            dve.wait_ge(hot_used[b], i + 1)
                        for u in range(width(b, last)):
                            c = b * BLOCK_COLS + u
                            here = ring[:, c * w:(c + 1) * w]
                            before = ring[:, (c - 1) * w:c * w] if c else carry[:, 0:w]
                            dve.wait_ge(scan_done, i * SCANS_STEP + (SCANS * l + c + 1))
                            dve.scalar_tensor_tensor(
                                out=here, in0=before, scalar=restart[:, bass.ds(i * RING_COLS + c, 1)],
                                in1=here, op0=ALU.add, op1=ALU.max).then_inc(scan_done, 1)
                            if l == 0:
                                dve.tensor_scalar(hot[:, c, 0:P], lane_bf[:, :],
                                                  dst_lane[:, bass.ds(i * RING_COLS + c, 1)], None,
                                                  ALU.is_equal).then_inc(hot_ready, 1)
                                dve.tensor_scalar(hot[:, c, P:HOT], lane_bf[:, 0:TILES],
                                                  dst_tile[:, bass.ds(i * RING_COLS + c, 1)], None,
                                                  ALU.is_equal).then_inc(hot_ready, 1)
                    columns = LAST if last else RING_COLS
                    dve.wait_ge(scan_done, i * SCANS_STEP + (SCANS * l + columns + 1))
                    dve.tensor_copy(carry[:, 0:w], ring[:, (columns - 1) * w:columns * w]
                                    ).then_inc(scan_done, 1)

                with dve.Fori(0, STEPS - 1) as i:
                    scan_step(i, False)
                scan_step(STEPS - 1, True)

                if l == 0:
                    dve.wait_ge(count_ready, 1)
                    dve.tensor_copy(count[:, :], hist_ps[:, 0:TILES]).then_inc(ends_step, 1)
                    dve.wait_ge(count_spread, 1)
                    dve.tensor_copy(total[:, :], hist_ps[:, TILES:2 * TILES]).then_inc(ends_step, 1)
                    dve.wait_ge(ends_step, 2)
                    dve.tensor_tensor_scan(upto[:, :], total[:, :], zero_tiles[:, :], 0.0,
                                           ALU.add, ALU.add).then_inc(ends_step, 1)
                    dve.wait_ge(ends_step, 3)
                    dve.tensor_tensor(total[:, :], upto[:, :], total[:, :], ALU.subtract).then_inc(ends_step, 1)
                    dve.wait_ge(ends_step, 4)
                    dve.scalar_tensor_tensor(out=ends[:, :], in0=hist_ps[:, 0:TILES],
                                             scalar=-float(1 + P * COLS), in1=total[:, :],
                                             op0=ALU.add, op1=ALU.add).then_inc(ends_step, 1)
                    dve.wait_ge(ends_step, 5)
                    dve.scalar_tensor_tensor(out=upto[:, :], in0=count[:, :], scalar=0.0,
                                             in1=ends[:, :], op0=ALU.is_gt, op1=ALU.mult).then_inc(ends_step, 1)
                    dve.wait_ge(ends_step, 6)
                    dve.tensor_scalar(end_row[:, 0:TILES], upto[:, :], float(P * COLS), None,
                                      ALU.add).then_inc(ends_step, 1)

                dve.wait_ge(carry_turned, l + 1)
                dve.wait_ge(join_diag, 3)
                for c in range(kc):
                    dve.tensor_tensor_scan(carry_scan[:, c, :], join_row[:, 1, :],
                                           carry_ps[:, c * P:(c + 1) * P], 0.0,
                                           ALU.add, ALU.max).then_inc(join_step, 1)
                for c in range(kc):
                    before = sum(s[0] for s in shapes[:l]) // P
                    dve.wait_ge(join_step, before + c + 1)
                    dve.tensor_tensor(incoming[:, c, 1:P], carry_scan[:, c, 0:P - 1],
                                      join_row[:, 0, 1:P], ALU.add).then_inc(incoming_ready, 1)
                dve.wait_ge(incoming_turned, l + 1)
                dve.wait_ge(patch_landed, DMA * (l + 1))
                dve.tensor_tensor(patch[:, 0:w], patch[:, 0:w], back_ps[:, 0:w], ALU.max).then_inc(patched, 1)

                def stage_ends(h, tile):
                    at = tile + SHARES[h]
                    size = SHARES[h + 1] - SHARES[h]
                    dve.tensor_copy(end_stage[h][:, :], end_row[:, bass.ds(at, size)]).then_inc(end_staged, 1)

                def mask(i, q):
                    b = BUFFERS[q % TAIL_PAIRS]
                    dve.wait_ge(agg_turned, i * TAIL_PAIRS + (PAIRS * l + q + 1))
                    dve.tensor_scalar(finite[b][:, 0:2 * w], turn_ps[b][:, 0:2 * w].bitcast(I32),
                                      TOP_EXPONENT, TOP_EXPONENT, ALU.bitwise_and, ALU.bitwise_xor
                                      ).then_inc(mask_done, 1)

                def guard(i, q):
                    b = BUFFERS[q % TAIL_PAIRS]
                    dve.wait_ge(mask_done, i * TAIL_PAIRS + (PAIRS * l + q + 1))
                    dve.wait_ge(agg_zeroed, i * TAIL_PAIRS + (PAIRS * l + q + 4 - REUSE[q % TAIL_PAIRS]))
                    dve.sem_inc(guard_open, 1)
                    dve.copy_predicated(agg[b][:, 0:2 * w], finite[b][:, 0:2 * w], turn_ps[b][:, 0:2 * w]
                                        ).then_inc(agg_done, 1)

                def add_own(i, q):
                    dve.wait_ge(z_ready, i * TAIL_PAIRS + (PAIRS * l + q + 1))
                    dve.tensor_tensor(z_sum[BUFFERS[q]][:, 0:2 * n], mm_ps[BUFFERS[q]][:, 0:2 * n],
                                      own[:, bass.ds(i * (TAIL_TILES * n) + q * (2 * n), 2 * n)],
                                      ALU.add).then_inc(sum_done, 1)

                def leaky(i, q):
                    made, z = h_out[q % TAIL_PAIRS], z_sum[BUFFERS[q % TAIL_PAIRS]]
                    dve.wait_ge(h_stored[q % TAIL_PAIRS], i * DMA + (PER_OUT * l + DMA * (1 + q // TAIL_PAIRS)))
                    dve.wait_ge(sum_done, i * TAIL_PAIRS + (PAIRS * l + q + 1))
                    dve.scalar_tensor_tensor(out=made[:, 0:2 * n], in0=z[:, 0:2 * n], scalar=SLOPE,
                                             in1=z[:, 0:2 * n], op0=ALU.mult, op1=ALU.max
                                             ).then_inc(h_done if l < LAYERS - 1 else act_done, 1)

                def residual(i, q):
                    if l == LAYERS - 1:
                        made = h_out[q % TAIL_PAIRS]
                        dve.wait_ge(act_done, i * TAIL_PAIRS + (q + 1))
                        dve.tensor_tensor(made[:, 0:2 * n], made[:, 0:2 * n],
                                          own[:, bass.ds(i * (TAIL_TILES * n) + (TILES * n + q * 2 * n), 2 * n)],
                                          ALU.add).then_inc(h_done, 1)

                dve.wait_ge(ends_step, ENDS)
                if l:
                    dve.wait_ge(end_staged, 2 * (TAIL_STEPS + 1) * l)
                stage_ends(0, 0)
                stage_ends(1, 0)
                dve.wait_ge(own_done, TILES * (l + 1))
                if l == LAYERS - 1:
                    dve.wait_ge(residual_loaded, DMA)

                def tail(i, first, last):
                    for q in range(1, TAIL_PAIRS + 1 - last):
                        mask(i, q)
                        if 2 * q + 2 in SHARES:
                            stage_ends(SHARES.index(2 * q + 2) - 1, i * TAIL_TILES + TAIL_TILES)
                        if q > 1 or not first:
                            leaky(i, q - 2)
                        guard(i, q)
                        add_own(i, q - 1)
                        if q > 1 or not first:
                            residual(i, q - 2)
                    if last:
                        leaky(i, TAIL_PAIRS - 2)
                        add_own(i, TAIL_PAIRS - 1)
                        residual(i, TAIL_PAIRS - 2)
                        leaky(i, TAIL_PAIRS - 1)
                        residual(i, TAIL_PAIRS - 1)

                mask(0, 0)
                guard(0, 0)
                tail(0, True, False)
                with dve.Fori(1, TAIL_STEPS - 1) as i:
                    tail(i, False, False)
                tail(TAIL_STEPS - 1, False, True)

        @block.tensor
        def _(pe):
            for b in range(BLOCKS):
                pe.sem_inc(hot_used[b], 1)
            for k in range(TAIL_PAIRS):
                pe.sem_inc(h_stored[k], DMA)
            pe.wait_ge(order_checked, 3)
            pe.matmul(back_ps[:, 0:1], ones[:, :], cols[:, 5:6], start=True, stop=True).then_inc(order_summed, 1)
            pe.wait_ge(join_diag, 2)
            for f in range(2):
                mm = pe.matmul(carry_ps[:, f * P:(f + 1) * P], ones[:, :], diag[:, f, :],
                               start=True, stop=True)
            mm.then_inc(join_spread, 1)
            pe.wait_ge(weights_loaded, N_WEIGHTS)

            for l, (w, n) in enumerate(shapes):
                kc = w // P

                def own_pair(j):
                    for p in range(2):
                        pe.wait_ge(in_loaded[p], j * DMA + DMA * (PAIRS * l + 1))
                        for c in range(kc):
                            turn = pe.transpose(turn_ps[p][:, c * P:(c + 1) * P],
                                                h_in[p][:, c * P:(c + 1) * P], ident[:, :])
                        turn.then_inc(in_turned, 1)
                        pe.wait_ge(in_copied, j * 2 + (TILES * l + p + 1))
                        for c in range(kc):
                            pe.matmul(mm_ps[p][:, 0:n], h_turned[p][:, c, :], wr_sb[l][:, c, :],
                                      start=(c == 0), stop=False)
                        pe.matmul(mm_ps[p][:, 0:n], ones[0:1, :], b_sb[l][:, :],
                                  start=False, stop=True).then_inc(own_mm, 1)

                def histogram(i, last):
                    for b in used_blocks(last):
                        pe.wait_ge(hot_ready, i * (2 * RING_COLS) + 2 * (b * BLOCK_COLS + width(b, last)))
                        for u in range(width(b, last)):
                            c = b * BLOCK_COLS + u
                            mm = pe.matmul(hist_ps[:, 0:TILES], hot[:, c, 0:P], hot[:, c, P:HOT],
                                           start=False, stop=False, skip_group_check=True)
                        mm.then_inc(hot_used[b], 1)

                if l == 0:
                    pe.wait_ge(const_done, CONSTS)
                    pe.matmul(hist_ps[:, 0:TILES], no_hot[:, 0:P], no_hot[:, P:HOT],
                              start=True, stop=False, skip_group_check=True)
                    with pe.Fori(0, PAIRS) as i:
                        histogram(i, False)
                        own_pair(i)
                    if STEPS - 1 > PAIRS:
                        with pe.Fori(PAIRS, STEPS - 1) as i:
                            histogram(i, False)
                    histogram(STEPS - 1, True)
                    pe.matmul(hist_ps[:, 0:TILES], no_hot[:, 0:P], no_hot[:, P:HOT],
                              start=False, stop=True, skip_group_check=True).then_inc(count_ready, 1)
                    pe.wait_ge(ends_step, 1)
                    pe.matmul(hist_ps[:, 0:TILES], upper[:, :], count[:, :], start=True, stop=True)
                    pe.matmul(hist_ps[:, TILES:2 * TILES], ones[:, :], count[:, :],
                              start=True, stop=True).then_inc(count_spread, 1)
                else:
                    with pe.Fori(0, PAIRS) as i:
                        own_pair(i)

                pe.wait_ge(scan_done, SCANS * (l + 1) + 1)
                for c in range(kc):
                    turn = pe.transpose(carry_ps[:, c * P:(c + 1) * P], carry[:, c * P:(c + 1) * P],
                                        ident[:, :])
                turn.then_inc(carry_turned, 1)
                pe.wait_ge(incoming_ready, sum(s[0] for s in shapes[:l + 1]) // P)
                for c in range(kc):
                    turn = pe.transpose(back_ps[:, c * P:(c + 1) * P], incoming[:, c, :], ident[:, :])
                turn.then_inc(incoming_turned, 1)

                def turn_pair(i, q):
                    b = BUFFERS[q % TAIL_PAIRS]
                    for t in range(2):
                        k = (2 * q + t) % TAIL_TILES
                        pe.wait_ge(end_landed[k], i * DMA + DMA * (TAIL_STEPS * l + q // TAIL_PAIRS + 1))
                        for c in range(kc):
                            turn = pe.transpose(turn_ps[b][:, t * w + c * P:t * w + (c + 1) * P],
                                                ring[:, k * w + c * P:k * w + (c + 1) * P], ident[:, :])
                    turn.then_inc(agg_turned, 1)

                def project_pair(i, q):
                    b = BUFFERS[q]
                    pe.wait_ge(agg_done, i * TAIL_PAIRS + (PAIRS * l + q + 1))
                    for t in range(2):
                        for c in range(kc):
                            mm = pe.matmul(mm_ps[b][:, t * n:(t + 1) * n],
                                           agg[b][:, t * w + c * P:t * w + (c + 1) * P],
                                           wl_sb[l][:, c, :], start=(c == 0), stop=(c == kc - 1))
                    mm.then_inc(z_ready, 1)

                def tail(i, last):
                    for q in range(1, TAIL_PAIRS + 1 - last):
                        turn_pair(i, q)
                        project_pair(i, q - 1)
                    if last:
                        project_pair(i, TAIL_PAIRS - 1)

                pe.wait_ge(own_done, TILES * (l + 1))
                turn_pair(0, 0)
                with pe.Fori(0, TAIL_STEPS - 1) as i:
                    tail(i, False)
                tail(TAIL_STEPS - 1, True)

        @block.scalar
        def _(act):
            def deviation(s):
                t = slice(s * TAIL_TILES, (s + 1) * TAIL_TILES)
                act.wait_ge(var_done, TAIL_TILES * (s + 1))
                nc.scalar.activation(std[:, t], mean_var[:, t, 1], ACT.Sqrt, bias=eps[:, 0:1]).then_inc(std_done, 1)

            act.wait_ge(const_done, CONSTS)
            deviation(0)
            for s in range(TAIL_STEPS):
                if s < TAIL_STEPS - 1:
                    deviation(s + 1)
                act.wait_ge(norm_ready, 2 * (s + 1))
                for k in range(s * TAIL_TILES, s * TAIL_TILES + ACT_TILES):
                    nc.scalar.activation(h0_all[:, k, :], x_all[:, k, :], ACT.Relu, bias=shift[:, k:k + 1],
                                         scale=rstd[:, k:k + 1]).then_inc(h0_done, 1)

            for b in range(3):
                nc.scalar.activation(agg[b][:, :], zeros[:, :], ACT.Copy).then_inc(agg_zeroed, 1)

            for l, (w, n) in enumerate(shapes):
                if l == 0:
                    act.wait_ge(h0_stored, DMA * TAIL_STEPS)
                else:
                    for b in range(TAIL_PAIRS):
                        act.wait_ge(h_stored[b], PER_OUT * l + DMA)
                if l == LAYERS - 1:
                    act.dma_start(own[:, TILES * n:TILES * (n + F_IN)].rearrange("p (t f) -> p t f", f=F_IN),
                                  x.rearrange("(t p) f -> p t f", p=P)).then_inc(residual_loaded, DMA)

                def load(tile, p):
                    act.dma_start(h_in[p][:, 0:w], tables[l][bass.ds(tile * P, P), :]).then_inc(in_loaded[p], DMA)

                def copy_pair(j, more):
                    for p in range(2):
                        act.wait_ge(in_turned, j * 2 + (TILES * l + p + 1))
                        nc.scalar.activation(h_turned[p][:, :, :].rearrange("p c m -> p (c m)")[:, 0:w],
                                             turn_ps[p][:, 0:w], ACT.Copy).then_inc(in_copied, 1)
                        if more:
                            load(j * 2 + (p + 2), p)
                        act.wait_ge(own_mm, j * 2 + (TILES * l + p + 1))
                        act.wait_ge(weights_loaded, N_WEIGHTS)
                        nc.scalar.activation(own[:, bass.ds(j * (2 * n) + p * n, n)], mm_ps[p][:, 0:n],
                                             ACT.Copy).then_inc(own_done, 1)

                load(0, 0)
                load(1, 1)
                with act.Fori(0, PAIRS - 1) as j:
                    copy_pair(j, True)
                copy_pair(PAIRS - 1, False)
                with act.Fori(0, TAIL_STEPS) as i:
                    for q in range(TAIL_PAIRS):
                        act.wait_ge(z_ready, i * TAIL_PAIRS + (PAIRS * l + q + 1))
                        nc.scalar.activation(agg[BUFFERS[q]][:, :], zeros[:, :], ACT.Copy).then_inc(agg_zeroed, 1)

        @block.sync
        def _(sp):
            x_rows = x.rearrange("(t p) f -> p t f", p=P)
            h0_rows = tables[0].rearrange("(t p) f -> p t f", p=P)
            for s in range(TAIL_STEPS):
                t = slice(s * TAIL_TILES, (s + 1) * TAIL_TILES)
                sp.dma_start(x_all[:, t, :], x_rows[:, t, :]).then_inc(x_loaded[s], DMA)
                if s == 0:
                    sp.dma_start(dst_t[:, :], dst).then_inc(edges_loaded, DMA)
                    with nc.allow_non_contiguous_dma(reason="one word of each partition's run of edges"):
                        sp.dma_start(prev_last[1:P, :], dst[0:P - 1, COLS - 1:COLS]).then_inc(edges_loaded, DMA)
            sp.dma_start(src_t[:, 0:COLS], src).then_inc(edges_loaded, DMA)
            for l, (wl, bl, wr) in enumerate(weights):
                sp.dma_start(wr_sb[l][:, :, :], wr.rearrange("(c p) n -> p c n", p=P)).then_inc(weights_loaded, DMA)
                sp.dma_start(wl_sb[l][:, :, :], wl.rearrange("(c p) n -> p c n", p=P)).then_inc(weights_loaded, DMA)
                sp.dma_start(b_sb[l][:, :], bl.rearrange("(a n) -> a n", a=1)).then_inc(weights_loaded, DMA)
            sp.wait_ge(const_done, CONSTS)
            for w in widths:
                sp.dma_start(logs[w][P * COLS:LOG_ROWS, :], empty_row[:, 0:w]).then_inc(empty_stored, DMA)
            for s in range(TAIL_STEPS):
                t = slice(s * TAIL_TILES, (s + 1) * TAIL_TILES)
                sp.wait_ge(h0_done, ACT_TILES * (s + 1))
                sp.wait_ge(h0_rest_done, s + 1)
                sp.dma_start(h0_rows[:, t, :], h0_all[:, t, :]).then_inc(h0_stored, DMA)

            for l, (w, n) in enumerate(shapes):

                def log_step(i, last):
                    for b in used_blocks(last):
                        c, columns = b * BLOCK_COLS, width(b, last)
                        sp.wait_ge(scan_done, i * SCANS_STEP + (SCANS * l + c + columns + 2))
                        sp.dma_start(log_block(l, i, b, columns), ring[:, c * w:(c + columns) * w]
                                     ).then_inc(logged[b], DMA)

                with sp.Fori(0, STEPS - 1) as i:
                    log_step(i, False)
                log_step(STEPS - 1, True)
                made = tables[l + 1] if l < LAYERS - 1 else out
                with sp.Fori(0, TAIL_STEPS) as i:
                    for q in range(TAIL_PAIRS):
                        sp.wait_ge(h_done, i * TAIL_PAIRS + (PAIRS * l + q + 1))
                        rows = made[bass.ds(i * (TAIL_TILES * P) + q * (2 * P), 2 * P), :]
                        sp.dma_start(rows.rearrange("(t p) f -> p t f", p=P),
                                     h_out[q][:, 0:2 * n].rearrange("p (t f) -> p t f", f=n)
                                     ).then_inc(h_stored[q], DMA)
            for b in range(TAIL_PAIRS):
                sp.wait_ge(h_stored[b], PER_OUT * LAYERS + DMA)


def kernel(**inputs):
    import numpy as np
    import concourse.bacc as bacc
    from concourse.bass_utils import run_bass_kernel_spmd

    x = np.ascontiguousarray(inputs["x"])
    nodes, features = x.shape
    edges = inputs["src"].shape[0]
    group = P * TAIL_TILES
    rows = -(-nodes // group) * group
    cols = -(-edges // P)

    def filled(a, size, fill):
        whole = np.full(size, fill, a.dtype)
        whole[:a.shape[0]] = a
        return whole.reshape(P, -1)

    x_rows = np.zeros((rows, features), x.dtype)
    x_rows[:nodes] = x
    arrays = {
        "x": x_rows,
        "src": filled(np.asarray(inputs["src"]), P * cols, 0),
        "dst": filled(np.asarray(inputs["dst"]), P * cols, NO_NODE),
    }
    layers = [f"L0_gnn_{part}{l}" for l in (1, 2, 3) for part in ("Wl", "bl", "Wr")]
    for name in layers:
        arrays[name] = np.ascontiguousarray(inputs[name])
    nc = bacc.Bacc("TRN2", target_bir_lowering=False, num_devices=1)
    given = {
        name: nc.dram_tensor(name, a.shape, mybir.dt.from_np(a.dtype), kind="ExternalInput").ap()
        for name, a in arrays.items()
    }
    out = nc.dram_tensor("out", (rows, arrays["L0_gnn_Wl3"].shape[1]), F32, kind="ExternalOutput").ap()
    weights = [tuple(given[name] for name in layers[3 * l:3 * l + 3]) for l in range(3)]
    gnn_program(nc, given["x"], given["src"], given["dst"], weights, out)
    r = run_bass_kernel_spmd(nc, [arrays], core_ids=[0])
    return r.results[0]["out"][:nodes]
```
